# Optimizing a Trainium2 kernel written in Bass

```python
import numpy as np
import jax
import jax.numpy as jnp

def _softmax(x, axis=-1):
    return jax.nn.softmax(x, axis=axis)

def _gelu(x):
    return jax.nn.gelu(x, approximate=True)

def _silu(x):
    return jax.nn.silu(x)

def _sigmoid(x):
    return jax.nn.sigmoid(x)

def _layernorm(x, axis=-1, eps=1e-05):
    m = jnp.mean(x, axis=axis, keepdims=True)
    v = jnp.var(x, axis=axis, keepdims=True)
    return (x - m) / jnp.sqrt(v + eps)

def _scatter_add(tgt, idx, src, axis=0):
    return tgt.at[idx].add(src)

def _segment_sum(src, seg, n):
    return jax.ops.segment_sum(src, seg, n)
kernel_name = 'mk_xattn_ffn_d1_seqx_r8_fd892e'

def setup_inputs(seed: int=0):
    np.random.seed(seed)
    _w = jnp.asarray

    def _rec_inputs():
        import jax
        import jax.numpy as jnp
        _rk = jax.random.key(seed)
        x = -0.0002928 + 1 * jax.random.normal(jax.random.fold_in(_rk, 1), (32, 64, 128), jnp.float32)
        _lenS = 64 - jax.random.randint(jax.random.fold_in(_rk, 7), (32,), 0, max(1, 64 // 4) + 1, jnp.int32)
        _lenS2 = 64 - jax.random.randint(jax.random.fold_in(_rk, 8), (32,), 0, max(1, 64 // 4) + 1, jnp.int32)
        _ctx_1024P = jax.random.normal(jax.random.fold_in(_rk, 11), (32, 16, 128), jnp.float32)
        _ctx_1024c = jax.random.dirichlet(jax.random.fold_in(_rk, 511), 0.3 * jnp.ones((16,), jnp.float32), (32, 64))
        _ctx_1024t = jnp.einsum('bsk,bkd->bsd', _ctx_1024c, _ctx_1024P)
        _ctx_1024t = _ctx_1024t * jax.lax.rsqrt(jnp.mean(jnp.square(_ctx_1024t)) + 1e-12) * 0.953939
        ctx_1024 = -1.39393e-06 + 0.999914 * (_ctx_1024t + 0.3 * jax.random.normal(jax.random.fold_in(_rk, 611), (32, 64, 128), jnp.float32))
        _validS = jnp.arange(64)[None, :] < _lenS[:, None]
        _validS2 = jnp.arange(64)[None, :] < _lenS2[:, None]
        _causal = jnp.tril(jnp.ones((64, 64), dtype=bool))
        mask_SxS2_ik0 = jnp.where(jnp.broadcast_to(_validS2[0:1, :], (64, 64)), 0, 1).astype(jnp.int32)
        mask_Bx1x1xS2_if1 = jnp.where(jnp.ones((32, 1, 1, 64), dtype=bool), 1, 0).astype(jnp.int32)
        return (x, ctx_1024, mask_SxS2_ik0, mask_Bx1x1xS2_if1)
    x, ctx_1024, mask_SxS2_ik0, mask_Bx1x1xS2_if1 = _rec_inputs()

    def _L0_xattn_setup():
        import jax, jax.numpy as jnp
        import numpy as np
        import math
        D_MODEL = 128
        N_HEADS = 16
        D_FF = 512
        D_K = D_MODEL // N_HEADS
        B, S_DEC, S_ENC = (2, 256, 256)
        EPS = 1e-05
        NEG = -1000000000.0

        def _linear(x, w, b):
            return jnp.einsum('bsi,io->bso', x, w) + b

        def _mha(xq, xkv, wq, bq, wk, bk, wv, bv, wo, bo, mask):
            b, sq, _ = xq.shape
            sk = xkv.shape[1]
            q = _linear(xq, wq, bq).reshape(b, sq, N_HEADS, D_K).transpose(0, 2, 1, 3)
            k = _linear(xkv, wk, bk).reshape(b, sk, N_HEADS, D_K).transpose(0, 2, 1, 3)
            v = _linear(xkv, wv, bv).reshape(b, sk, N_HEADS, D_K).transpose(0, 2, 1, 3)
            scores = jnp.einsum('bhqd,bhkd->bhqk', q, k) / math.sqrt(D_K)
            if mask is not None:
                scores = jnp.where(mask == 0, NEG, scores)
            attn = jax.nn.softmax(scores, axis=-1)
            out = jnp.einsum('bhqk,bhkd->bhqd', attn, v)
            out = out.transpose(0, 2, 1, 3).reshape(b, sq, D_MODEL)
            return _linear(out, wo, bo)

        def _layernorm(x, gamma, beta):
            mean = jnp.mean(x, axis=-1, keepdims=True)
            std = jnp.sqrt(jnp.mean((x - mean) ** 2, axis=-1, keepdims=True))
            return (x - mean) / (std + EPS) * gamma + beta
        key = jax.random.key(seed)
        ks = jax.random.split(key, 24)
        sc = 1.0 / math.sqrt(D_MODEL)

        def W(k, i, o):
            return jax.random.normal(k, (i, o), jnp.float32) * sc
        inp = {'x': jax.random.normal(ks[0], (B, S_DEC, D_MODEL), jnp.float32), 'encoder_output': jax.random.normal(ks[1], (B, S_ENC, D_MODEL), jnp.float32), 'causal_mask': jnp.tril(jnp.ones((S_DEC, S_DEC), jnp.int32)), 'padding_mask': jnp.ones((B, 1, 1, S_ENC), jnp.int32), 'sa_wq': W(ks[2], D_MODEL, D_MODEL), 'sa_bq': jnp.zeros(D_MODEL), 'sa_wk': W(ks[3], D_MODEL, D_MODEL), 'sa_bk': jnp.zeros(D_MODEL), 'sa_wv': W(ks[4], D_MODEL, D_MODEL), 'sa_bv': jnp.zeros(D_MODEL), 'sa_wo': W(ks[5], D_MODEL, D_MODEL), 'sa_bo': jnp.zeros(D_MODEL), 'ca_wq': W(ks[6], D_MODEL, D_MODEL), 'ca_bq': jnp.zeros(D_MODEL), 'ca_wk': W(ks[7], D_MODEL, D_MODEL), 'ca_bk': jnp.zeros(D_MODEL), 'ca_wv': W(ks[8], D_MODEL, D_MODEL), 'ca_bv': jnp.zeros(D_MODEL), 'ca_wo': W(ks[9], D_MODEL, D_MODEL), 'ca_bo': jnp.zeros(D_MODEL), 'ff_w1': W(ks[10], D_MODEL, D_FF), 'ff_b1': jnp.zeros(D_FF), 'ff_w2': jax.random.normal(ks[11], (D_FF, D_MODEL), jnp.float32) / math.sqrt(D_FF), 'ff_b2': jnp.zeros(D_MODEL), 'g1': jnp.ones(D_MODEL), 'b1': jnp.zeros(D_MODEL), 'g2': jnp.ones(D_MODEL), 'b2': jnp.zeros(D_MODEL), 'g3': jnp.ones(D_MODEL), 'b3': jnp.zeros(D_MODEL)}
        return inp
    _L0_xattn_all = _L0_xattn_setup()
    _L0_xattn_in = {k: v for k, v in _L0_xattn_all.items() if k in ('sa_wq', 'sa_bq', 'sa_wk', 'sa_bk', 'sa_wv', 'sa_bv', 'sa_wo', 'sa_bo', 'ca_wq', 'ca_bq', 'ca_wk', 'ca_bk', 'ca_wv', 'ca_bv', 'ca_wo', 'ca_bo', 'ff_w1', 'ff_b1', 'ff_w2', 'ff_b2', 'g1', 'b1', 'g2', 'b2', 'g3', 'b3')}
    del _L0_xattn_all

    def _L0_ffn_setup():
        import jax, jax.numpy as jnp
        import numpy as np
        from jax import lax
        H = 128
        E = 8
        E_MLP = E - 4
        TOP_K = 2
        I = 64
        KC = 4
        SHARED_SCALE = 1.0
        key = jax.random.key(seed)
        ks = jax.random.split(key, 8)
        B, S = (4, 512)
        s_h = 1.0 / np.sqrt(H)
        s_i = 1.0 / np.sqrt(I)
        return {'hidden_states': jax.random.normal(ks[0], (B, S, H), dtype=jnp.float32), 'Wr': jax.random.normal(ks[1], (H, E), dtype=jnp.float32) * s_h, 'router_bias': jnp.zeros((E,), dtype=jnp.float32), 'Wg': jax.random.normal(ks[2], (E_MLP, H, I), dtype=jnp.float32) * s_h, 'Wu': jax.random.normal(ks[3], (E_MLP, H, I), dtype=jnp.float32) * s_h, 'Wd': jax.random.normal(ks[4], (E_MLP, I, H), dtype=jnp.float32) * s_i, 'conv_w': jax.random.normal(ks[5], (KC, 1, H), dtype=jnp.float32) * (1.0 / np.sqrt(KC)), 'conv_b': jnp.zeros((H,), dtype=jnp.float32)}
    _L0_ffn_all = _L0_ffn_setup()
    _L0_ffn_in = {k: v for k, v in _L0_ffn_all.items() if k in ('Wr', 'router_bias', 'Wg', 'Wu', 'Wd', 'conv_w', 'conv_b')}
    del _L0_ffn_all
    return {'x': x, 'ctx_1024': ctx_1024, 'mask_SxS2_ik0': mask_SxS2_ik0, 'mask_Bx1x1xS2_if1': mask_Bx1x1xS2_if1, 'L0_xattn_sa_wq': _L0_xattn_in['sa_wq'], 'L0_xattn_sa_bq': _L0_xattn_in['sa_bq'], 'L0_xattn_sa_wk': _L0_xattn_in['sa_wk'], 'L0_xattn_sa_bk': _L0_xattn_in['sa_bk'], 'L0_xattn_sa_wv': _L0_xattn_in['sa_wv'], 'L0_xattn_sa_bv': _L0_xattn_in['sa_bv'], 'L0_xattn_sa_wo': _L0_xattn_in['sa_wo'], 'L0_xattn_sa_bo': _L0_xattn_in['sa_bo'], 'L0_xattn_ca_wq': _L0_xattn_in['ca_wq'], 'L0_xattn_ca_bq': _L0_xattn_in['ca_bq'], 'L0_xattn_ca_wk': _L0_xattn_in['ca_wk'], 'L0_xattn_ca_bk': _L0_xattn_in['ca_bk'], 'L0_xattn_ca_wv': _L0_xattn_in['ca_wv'], 'L0_xattn_ca_bv': _L0_xattn_in['ca_bv'], 'L0_xattn_ca_wo': _L0_xattn_in['ca_wo'], 'L0_xattn_ca_bo': _L0_xattn_in['ca_bo'], 'L0_xattn_ff_w1': _L0_xattn_in['ff_w1'], 'L0_xattn_ff_b1': _L0_xattn_in['ff_b1'], 'L0_xattn_ff_w2': _L0_xattn_in['ff_w2'], 'L0_xattn_ff_b2': _L0_xattn_in['ff_b2'], 'L0_xattn_g1': _L0_xattn_in['g1'], 'L0_xattn_b1': _L0_xattn_in['b1'], 'L0_xattn_g2': _L0_xattn_in['g2'], 'L0_xattn_b2': _L0_xattn_in['b2'], 'L0_xattn_g3': _L0_xattn_in['g3'], 'L0_xattn_b3': _L0_xattn_in['b3'], 'L0_ffn_Wr': _L0_ffn_in['Wr'], 'L0_ffn_router_bias': _L0_ffn_in['router_bias'], 'L0_ffn_Wg': _L0_ffn_in['Wg'], 'L0_ffn_Wu': _L0_ffn_in['Wu'], 'L0_ffn_Wd': _L0_ffn_in['Wd'], 'L0_ffn_conv_w': _L0_ffn_in['conv_w'], 'L0_ffn_conv_b': _L0_ffn_in['conv_b']}

def reference(x, ctx_1024, mask_SxS2_ik0, mask_Bx1x1xS2_if1, L0_xattn_sa_wq, L0_xattn_sa_bq, L0_xattn_sa_wk, L0_xattn_sa_bk, L0_xattn_sa_wv, L0_xattn_sa_bv, L0_xattn_sa_wo, L0_xattn_sa_bo, L0_xattn_ca_wq, L0_xattn_ca_bq, L0_xattn_ca_wk, L0_xattn_ca_bk, L0_xattn_ca_wv, L0_xattn_ca_bv, L0_xattn_ca_wo, L0_xattn_ca_bo, L0_xattn_ff_w1, L0_xattn_ff_b1, L0_xattn_ff_w2, L0_xattn_ff_b2, L0_xattn_g1, L0_xattn_b1, L0_xattn_g2, L0_xattn_b2, L0_xattn_g3, L0_xattn_b3, L0_ffn_Wr, L0_ffn_router_bias, L0_ffn_Wg, L0_ffn_Wu, L0_ffn_Wd, L0_ffn_conv_w, L0_ffn_conv_b):
    import jax
    import jax.numpy as jnp

    def _L0_xattn_ref(x, encoder_output, causal_mask, padding_mask, sa_wq, sa_bq, sa_wk, sa_bk, sa_wv, sa_bv, sa_wo, sa_bo, ca_wq, ca_bq, ca_wk, ca_bk, ca_wv, ca_bv, ca_wo, ca_bo, ff_w1, ff_b1, ff_w2, ff_b2, g1, b1, g2, b2, g3, b3):
        import jax, jax.numpy as jnp
        import numpy as np
        import math
        D_MODEL = 128
        N_HEADS = 16
        D_FF = 512
        D_K = D_MODEL // N_HEADS
        B, S_DEC, S_ENC = (2, 256, 256)
        EPS = 1e-05
        NEG = -1000000000.0

        def _linear(x, w, b):
            return jnp.einsum('bsi,io->bso', x, w) + b

        def _mha(xq, xkv, wq, bq, wk, bk, wv, bv, wo, bo, mask):
            b, sq, _ = xq.shape
            sk = xkv.shape[1]
            q = _linear(xq, wq, bq).reshape(b, sq, N_HEADS, D_K).transpose(0, 2, 1, 3)
            k = _linear(xkv, wk, bk).reshape(b, sk, N_HEADS, D_K).transpose(0, 2, 1, 3)
            v = _linear(xkv, wv, bv).reshape(b, sk, N_HEADS, D_K).transpose(0, 2, 1, 3)
            scores = jnp.einsum('bhqd,bhkd->bhqk', q, k) / math.sqrt(D_K)
            if mask is not None:
                scores = jnp.where(mask == 0, NEG, scores)
            attn = jax.nn.softmax(scores, axis=-1)
            out = jnp.einsum('bhqk,bhkd->bhqd', attn, v)
            out = out.transpose(0, 2, 1, 3).reshape(b, sq, D_MODEL)
            return _linear(out, wo, bo)

        def _layernorm(x, gamma, beta):
            mean = jnp.mean(x, axis=-1, keepdims=True)
            std = jnp.sqrt(jnp.mean((x - mean) ** 2, axis=-1, keepdims=True))
            return (x - mean) / (std + EPS) * gamma + beta
        sa = _mha(x, x, sa_wq, sa_bq, sa_wk, sa_bk, sa_wv, sa_bv, sa_wo, sa_bo, causal_mask)
        x = _layernorm(x + sa, g1, b1)
        ca = _mha(x, encoder_output, ca_wq, ca_bq, ca_wk, ca_bk, ca_wv, ca_bv, ca_wo, ca_bo, padding_mask)
        x = _layernorm(x + ca, g2, b2)
        h = jax.nn.relu(_linear(x, ff_w1, ff_b1))
        ff = _linear(h, ff_w2, ff_b2)
        x = _layernorm(x + ff, g3, b3)
        return x

    def _L0_ffn_ref(hidden_states, Wr, router_bias, Wg, Wu, Wd, conv_w, conv_b):
        import jax, jax.numpy as jnp
        import numpy as np
        from jax import lax
        H = 128
        E = 8
        E_MLP = E - 4
        TOP_K = 2
        I = 64
        KC = 4
        SHARED_SCALE = 1.0
        B, S, Hd = hidden_states.shape
        T = B * S
        x = hidden_states.reshape(T, Hd)
        scores = jax.nn.sigmoid(x @ Wr)
        _, idx = lax.top_k(scores + router_bias, TOP_K)
        w = jnp.take_along_axis(scores, idx, axis=-1)
        w = w / (jnp.sum(w, axis=-1, keepdims=True) + 1e-09)
        cw = jnp.zeros((T, E), dtype=x.dtype).at[jnp.arange(T)[:, None], idx].add(w)
        g = jnp.einsum('th,ehi->tei', x, Wg)
        u = jnp.einsum('th,ehi->tei', x, Wu)
        hid = jax.nn.silu(g) * u
        mlp_out = jnp.einsum('tei,eih->teh', hid, Wd)
        routed = jnp.einsum('te,teh->th', cw[:, :E_MLP], mlp_out)
        routed = routed + cw[:, E_MLP:E_MLP + 1] * x
        routed = routed + cw[:, E_MLP + 2:E_MLP + 3] * x
        routed = routed + cw[:, E_MLP + 3:E_MLP + 4] * jax.nn.relu(x)
        routed = routed.reshape(B, S, Hd)
        shared = lax.conv_general_dilated(hidden_states, conv_w, window_strides=(1,), padding=[(KC - 1, 0)], dimension_numbers=('NHC', 'HIO', 'NHC'), feature_group_count=Hd) + conv_b
        return routed + SHARED_SCALE * shared
    x = x + _L0_xattn_ref(_layernorm(x, axis=-1), ctx_1024, mask_SxS2_ik0, mask_Bx1x1xS2_if1, L0_xattn_sa_wq, L0_xattn_sa_bq, L0_xattn_sa_wk, L0_xattn_sa_bk, L0_xattn_sa_wv, L0_xattn_sa_bv, L0_xattn_sa_wo, L0_xattn_sa_bo, L0_xattn_ca_wq, L0_xattn_ca_bq, L0_xattn_ca_wk, L0_xattn_ca_bk, L0_xattn_ca_wv, L0_xattn_ca_bv, L0_xattn_ca_wo, L0_xattn_ca_bo, L0_xattn_ff_w1, L0_xattn_ff_b1, L0_xattn_ff_w2, L0_xattn_ff_b2, L0_xattn_g1, L0_xattn_b1, L0_xattn_g2, L0_xattn_b2, L0_xattn_g3, L0_xattn_b3)
    x = x + _L0_ffn_ref(_layernorm(x, axis=-1), L0_ffn_Wr, L0_ffn_router_bias, L0_ffn_Wg, L0_ffn_Wu, L0_ffn_Wd, L0_ffn_conv_w, L0_ffn_conv_b)
    return x

_drawn_inputs = setup_inputs


def setup_inputs(seed=0):
    import zlib

    import numpy as np

    out = dict(_drawn_inputs(seed))
    spreads = {'L0_xattn_sa_bq': (0.0, 0.295),
     'L0_xattn_sa_bk': (0.0, 2.0),
     'L0_xattn_sa_bv': (0.0, 0.1),
     'L0_xattn_sa_bo': (0.0, 0.1),
     'L0_xattn_ca_bq': (0.0, 0.359),
     'L0_xattn_ca_bk': (0.0, 2.0),
     'L0_xattn_ca_bv': (0.0, 0.1),
     'L0_xattn_ca_bo': (0.0, 0.1),
     'L0_xattn_ff_b1': (0.0, 0.1),
     'L0_xattn_ff_b2': (0.0, 0.1),
     'L0_xattn_g1': (1.0, 0.2),
     'L0_xattn_b1': (0.0, 0.1),
     'L0_xattn_g2': (1.0, 0.2),
     'L0_xattn_b2': (0.0, 0.1),
     'L0_xattn_g3': (1.0, 0.2),
     'L0_xattn_b3': (0.0, 0.1),
     'L0_ffn_router_bias': (0.0, 0.1),
     'L0_ffn_conv_b': (0.0, 0.1)}
    factors = {}
    for name, (base, spread) in spreads.items():
        noise = np.random.default_rng([zlib.crc32(name.encode()), seed]).standard_normal(out[name].shape)
        drawn = base * np.exp(spread * noise) if base else spread * noise
        out[name] = jnp.asarray(drawn.astype(out[name].dtype))
    for name, factor in factors.items():
        out[name] = (out[name] * factor).astype(out[name].dtype)
    return out
```

```python
from contextlib import ExitStack

import concourse.bass as bass
from concourse import mybir

F32 = mybir.dt.float32
BF16 = mybir.dt.bfloat16
I32 = mybir.dt.int32
U32 = mybir.dt.uint32
ALU = mybir.AluOpType
ACT = mybir.ActivationFunctionType
AX_X = mybir.AxisListType.X

P = 128
SEQ = 64
HEADS, DK = 16, 8
PAIRS = 2
TOK = PAIRS * P
BATCH = TOK // SEQ
ROWS = 4
HR = HEADS // ROWS
FF = 4
EXP, INNER = 4, 64
NE = 8
TAPS = 4
VW = DK + 1
NEG = -float(2 ** 100)
EPS = 1e-5

COLS = ["sa_bq", "sa_bk", "sa_bv", "ca_bq", "ca_bk", "ca_bv", "g1", "b1", "g2", "b2",
        "ff0", "ff1", "ff2", "ff3", "tap0", "tap1", "tap2", "tap3"]
ROWV = ["sa_bo", "g1", "b1", "ca_bo", "g2", "b2", "ff_b2", "g3", "b3", "conv_b"]
C_ID, C_HEAD, C_IOTA, C_PAIR, C_POW = 0, P, P + HR, P + HR + NE, P + HR + NE + P
C_END = C_POW + 2 * PAIRS


def program(nc, x, ctx, mask_self, mask_cross, wq_s, wk_s, wv_s, wo_s, wq_c, wk_c, wv_c, wo_c,
            w1, w2, wr, wg, wu, wd, cols_d, rows_d, rb_d, const_d, out):
    GROUPS = x.shape[0] * SEQ // TOK
    SCALE = float(DK) ** -0.5

    def by_group(a):
        return a.rearrange("b s d -> (b s) d").rearrange("(g p t) d -> g t p d", p=PAIRS, t=P)

    x_g, ctx_g, out_g = by_group(x), by_group(ctx), by_group(out)

    with ExitStack() as stack:
        def sb(name, shape, dt=F32):
            return stack.enter_context(nc.sbuf_tensor(name, shape, dt))

        def sem(name):
            return stack.enter_context(nc.semaphore(name))

        bank = [stack.enter_context(nc.psum_tensor(f"bank{i}", [P, 512], F32)) for i in range(8)]
        S_BANK, PT_BANK = bank[0:2], bank[2:4]
        O_BANK, PROJ, POST, FFB = bank[4:8]

        w = {"S": {}, "C": {}}
        for ph in "SC":
            for n in ("q", "k", "v", "o"):
                w[ph][n] = sb(f"w{n}_{ph}", [P, P])
        w1_sb = sb("w1_sb", [P, FF * P])
        w2_sb = sb("w2_sb", [P, FF, P])
        wr_sb = sb("wr_sb", [P, NE])
        wgu_sb = sb("wgu_sb", [P, 2, EXP, INNER])
        wd_sb = sb("wd_sb", [P, 2, P])
        cols = sb("cols", [P, len(COLS)])
        rows = sb("rows", [P, len(ROWV), P])
        rb = sb("rb", [P, NE])
        const = sb("const", [P, C_END])
        msk_s = sb("msk_s", [SEQ, SEQ], I32)
        msk_c = sb("msk_c", [2, GROUPS * PAIRS, SEQ], I32)
        neg_s = sb("neg_s", [SEQ, SEQ], BF16)
        neg_c = sb("neg_c", [2, GROUPS * PAIRS, SEQ], BF16)
        pick_s = sb("pick_s", [SEQ, P], BF16)
        pick_c = sb("pick_c", [2, P], BF16)
        bqs = sb("bqs", [P, 2])
        bkh = {ph: sb(f"bkh_{ph}", [P, HR]) for ph in "SC"}
        diag = sb("diag", [P, TAPS, P])
        res1_b = sb("res1_b", [P, P])
        res2_b = sb("res2_b", [P, P])
        ident = const[:, C_ID:C_ID + P]
        headmask = const[:, C_HEAD:C_HEAD + HR]
        iota8 = const[:, C_IOTA:C_IOTA + NE]

        def col(name):
            return cols[:, COLS.index(name):COLS.index(name) + 1]

        def row(name):
            return rows[:, ROWV.index(name), :]

        def pairs(r, n=PAIRS):
            return r.rearrange("p (a m) -> p a m", a=1).broadcast_to([P, n, r.shape[1]])

        x_tm = sb("x_tm", [P, PAIRS, P])
        ctx_tm = sb("ctx_tm", [P, PAIRS, P])
        xres = sb("xres", [P, PAIRS, P])
        xn = sb("xn", [P, PAIRS, P])
        src_fm = {"S": sb("xnT", [P, TOK]), "C": sb("x1T", [P, TOK])}
        encT = sb("encT", [P, TOK])
        kv_fm = {"S": src_fm["S"], "C": encT}
        x2T = sb("x2T", [P, TOK])
        qz = {ph: sb(f"qz_{ph}", [P, ROWS, TOK]) for ph in "SC"}
        kbd = {ph: sb(f"kbd_{ph}", [P, HR, TOK]) for ph in "SC"}
        vbd = {ph: sb(f"vbd_{ph}", [P, BATCH, HEADS // 2, 2, VW]) for ph in "SC"}
        rowmax = sb("rowmax", [P, 2, 8])
        prob = sb("prob", [P, 2, 512])
        probT = sb("probT", [P, 2, 512])
        rsum = {ph: sb(f"rsum_{ph}", [P, 2 * HEADS]) for ph in "SC"}
        o_tm = {ph: sb(f"o_tm_{ph}", [P, PAIRS, P]) for ph in "SC"}
        oT = {ph: sb(f"oT_{ph}", [P, TOK]) for ph in "SC"}
        LN = ("pre", "S", "C", "3", "4")
        y = {n: sb(f"y_{n}", [P, PAIRS, P]) for n in ("S", "C", "3")}
        z = {n: sb(f"z_{n}", [P, PAIRS, P]) for n in ("S", "C", "3", "4")}
        res = {n: sb(f"res_{n}", [P, PAIRS, P]) for n in ("S", "C", "3")}
        stats = {n: sb(f"stats_{n}", [P, PAIRS, 6]) for n in LN}
        mv = {n: sb(f"mv_{n}", [P, PAIRS, 2]) for n in LN}
        var = {n: sb(f"var_{n}", [P, PAIRS]) for n in LN}
        root = {n: sb(f"root_{n}", [P, PAIRS]) for n in LN}
        inv = {n: sb(f"inv_{n}", [P, PAIRS]) for n in LN}
        hT = sb("hT", [P, FF, TOK])
        xb3 = sb("xb3", [P, PAIRS, P])
        xnew = sb("xnew", [P, PAIRS, P])
        xnc = sb("xnc", [P, PAIRS, P])
        z4T = sb("z4T", [P, BATCH, TAPS - 1 + SEQ])
        e_r = sb("e_r", [P, PAIRS, NE])
        score = sb("score", [P, PAIRS, NE])
        biased = sb("biased", [P, PAIRS, NE])
        top = sb("top", [P, PAIRS, 8])
        topi = sb("topi", [P, PAIRS, 8], U32)
        topf = sb("topf", [P, PAIRS, 2])
        pick0 = sb("pick0", [P, PAIRS, NE])
        pick1 = sb("pick1", [P, PAIRS, NE])
        chosen = sb("chosen", [P, PAIRS, NE])
        wsum = sb("wsum", [P, PAIRS])
        cw = sb("cw", [P, PAIRS, NE])
        cwh = sb("cwh", [P, PAIRS, EXP])
        c46 = sb("c46", [P, PAIRS])
        th = sb("th", [P, PAIRS, EXP * INNER])
        sig = sb("sig", [P, PAIRS, EXP * INNER])
        hid = sb("hid", [P, PAIRS, EXP * INNER])
        hidc = sb("hidc", [P, PAIRS, EXP * INNER])
        hidT = sb("hidT", [P, PAIRS, 2, P])
        pass_x = sb("pass_x", [P, PAIRS, P])
        pass_r = sb("pass_r", [P, PAIRS, P])
        rest = sb("rest", [P, PAIRS, P])
        y_out = sb("y_out", [P, PAIRS, P])

        small_loaded = sem("small_loaded")
        proj_loaded, ffn_loaded, mix_loaded = sem("proj_loaded"), sem("ffn_loaded"), sem("mix_loaded")
        x_loaded, ctx_loaded, xres_loaded, stored = (sem(n) for n in
                                                     ("x_loaded", "ctx_loaded", "xres_loaded", "stored"))
        dve_setup, pool_setup, setup_step = sem("dve_setup"), sem("pool_setup"), sem("setup_step")

        def both(name):
            return {ph: sem(f"{name}_{ph}") for ph in "SC"}

        scores_done, max_done, shift_done, exp_done = (both(n) for n in ("scores", "max", "shift", "exp"))
        probT_done, probT_copied, pv_done = (both(n) for n in ("probT", "probTc", "pv"))
        qk_done, v_done, kbd_ready, vbd_ready = (both(n) for n in ("qk", "v", "kbd", "vbd"))
        osum_step, o_ready, oT_done, oT_ready = (both(n) for n in ("osum", "o", "oTps", "oT"))
        y_done = {n: sem(f"yps_{n}") for n in ("S", "C", "3")}
        y_ready = {n: sem(f"y_{n}r") for n in ("S", "C", "3")}
        res_step = {n: sem(f"res_step_{n}") for n in ("S", "C", "3")}
        res_ready = {n: sem(f"res_{n}r") for n in ("S", "C", "3")}
        stats_done = {n: sem(f"stats_{n}d") for n in LN}
        mean_done = {n: sem(f"mean_{n}d") for n in LN}
        var_ready = {n: sem(f"var_{n}r") for n in LN}
        root_ready = {n: sem(f"root_{n}r") for n in LN}
        inv_step = {n: sem(f"inv_step_{n}") for n in LN}
        z_ready = {n: sem(f"z_{n}r") for n in LN}
        zT_done = {n: sem(f"zTps_{n}") for n in LN}
        zT_ready = {n: sem(f"zT_{n}r") for n in LN}
        encT_done, encT_ready = sem("encTps"), sem("encT_ready")
        h_done = [sem("h_ps0"), sem("h_ps1")]
        h_ready = [sem("h_ready0"), sem("h_ready1")]
        xb3_ready, xz_step, xnew_ready, xnc_ready = (sem(n) for n in ("xb3", "xz_step", "xnew_r", "xnc_r"))
        logits_done, er_ready, route_step, cw_ready = (sem(n) for n in ("logits", "er", "route_step", "cw"))
        biased_done, top_done, topi_done = sem("biased_d"), sem("top_d"), sem("topi_d")
        gu_done = [sem("gu_ps0"), sem("gu_ps1")]
        th_ready = [sem("th0"), sem("th1")]
        gate_step = [sem("gate_step0"), sem("gate_step1")]
        hid_ready = [sem("hid0"), sem("hid1")]
        hidc_ready = [sem("hidc0"), sem("hidc1")]
        hidT_done, hidT_ready, acc_done = sem("hidTps"), sem("hidT_ready"), sem("acc")
        pass_ready, rest_ready, out_ready = sem("pass_r_sem"), sem("rest_sem"), sem("out_sem")

        def live(g):
            return not isinstance(g, int) or 0 <= g < GROUPS

        def follows(g):
            return not isinstance(g, int) or g >= 1

        def slot(t, c):
            if c < 0:
                t, c = t - 1, c + 2 * ROWS
            return ("S", t, c) if c < ROWS else ("C", t - 1, c - ROWS)

        def two_back(ph, g, r):
            if r >= 2:
                return ph, ROWS * g + r - 1
            other, og = ("C", g - 2) if ph == "S" else ("S", g + 1)
            if not live(og):
                other, og = ph, g - 1
            return (other, ROWS * og + r + 3) if live(og) else None

        def parity(r):
            return r % 2

        PROJ_USES = [(kbd_ready["C"], -1), (vbd_ready["C"], -1), (hid_ready[1], -3), (kbd_ready["S"], 1),
                     (vbd_ready["S"], 1), (hidT_ready, -3)]
        POST_USES = [(encT_ready, -1), (zT_ready["S"], -1), (oT_ready["C"], -2), (y_ready["C"], -2),
                     (zT_ready["pre"], 1), (zT_ready["C"], -2), (oT_ready["S"], 0), (y_ready["S"], 0)]
        FFB_USES = [(y_ready["3"], -3), (out_ready, -4), (zT_ready["4"], -3), (er_ready, -3),
                    (hid_ready[0], -3), (h_ready[0], -2), (h_ready[1], -2)]

        def last_read(uses, n, t):
            for back in range(1, len(uses) + 1):
                m = n - back
                s, off = uses[m % len(uses)]
                g = t + off - (1 if m < 0 else 0)
                if live(g):
                    return s, g + 1
            return None

        def settle(eng):
            eng.wait_ge(small_loaded, 96)

        block = stack.enter_context(nc.Block())

        def run(eng, iteration):
            first, last = 4, GROUPS - 2
            for t in range(-1, first):
                iteration(t)
            with eng.Fori(first, last) as t:
                iteration(t)
            for t in range(last, GROUPS + 4):
                iteration(t)

        @block.sync
        def _(sp):
            def load_x(g):
                if follows(g):
                    sp.wait_ge(z_ready["pre"], g)
                sp.dma_start(x_tm[:], x_g[g]).then_inc(x_loaded, 16)

            def load_ctx(g):
                if follows(g):
                    sp.wait_ge(encT_done, g)
                sp.dma_start(ctx_tm[:], ctx_g[g]).then_inc(ctx_loaded, 16)

            def load_xres(g):
                if follows(g):
                    sp.wait_ge(xb3_ready, g)
                sp.dma_start(xres[:], x_g[g]).then_inc(xres_loaded, 16)

            load_x(0)
            sp.dma_start(const[:], const_d).then_inc(small_loaded, 16)
            sp.dma_start(cols[:], cols_d).then_inc(small_loaded, 16)
            for n, a in (("q", wq_s), ("k", wk_s), ("v", wv_s), ("o", wo_s)):
                sp.dma_start(w["S"][n][:], a).then_inc(proj_loaded, 16)
            sp.dma_start(msk_s[:], mask_self).then_inc(small_loaded, 16)
            sp.dma_start(msk_c[:], mask_cross.rearrange("(t b) i j k -> b t (i j k)", b=2)).then_inc(small_loaded, 16)
            sp.dma_start(rows[:].rearrange("p a m -> p (a m)"),
                         rows_d.broadcast_to([P, len(ROWV) * P])).then_inc(small_loaded, 16)
            sp.dma_start(rb[:], rb_d.broadcast_to([P, NE])).then_inc(small_loaded, 16)
            for n, a in (("q", wq_c), ("k", wk_c), ("v", wv_c), ("o", wo_c)):
                sp.dma_start(w["C"][n][:], a).then_inc(proj_loaded, 16)
            sp.dma_start(w1_sb[:], w1).then_inc(ffn_loaded, 16)
            sp.dma_start(w2_sb[:], w2.rearrange("(c p) n -> p c n", p=P)).then_inc(ffn_loaded, 16)
            sp.dma_start(wr_sb[:], wr).then_inc(mix_loaded, 16)
            sp.dma_start(wgu_sb[:, 0], wg.rearrange("e h i -> h e i")).then_inc(mix_loaded, 16)
            sp.dma_start(wgu_sb[:, 1], wu.rearrange("e h i -> h e i")).then_inc(mix_loaded, 16)
            sp.dma_start(wd_sb[:], wd.rearrange("(c e) i h -> (e i) c h", c=2)).then_inc(mix_loaded, 16)

            def iteration(t):
                if live(t - 4):
                    sp.wait_ge(out_ready, t - 3)
                    sp.dma_start(out_g[t - 4], y_out[:]).then_inc(stored, 16)
                if live(t - 3):
                    load_xres(t - 3)
                if live(t + 2):
                    load_x(t + 2)
                if live(t):
                    load_ctx(t)

            run(sp, iteration)
            sp.wait_ge(stored, 16 * GROUPS)

        @block.gpsimd
        def _(pool):
            for ph in "SC":
                nc.gpsimd.memset(qz[ph][:], 0.0)
                nc.gpsimd.memset(vbd[ph][:], 0.0)
            nc.gpsimd.memset(z4T[:], 0.0).then_inc(setup_step, 1)
            pool.wait_ge(setup_step, 1)
            for ph in "SC":
                nc.gpsimd.memset(vbd[ph][0:SEQ, :, :, 0, DK:VW], 1.0)
                nc.gpsimd.memset(vbd[ph][SEQ:P, :, :, 1, DK:VW], 1.0).then_inc(pool_setup, 1)
            pool.wait_ge(pool_setup, 2)
            pool.wait_ge(small_loaded, 96)
            nc.gpsimd.tensor_tensor(res1_b[:], row("b1"), row("ca_bo"), ALU.add)
            nc.gpsimd.tensor_tensor(res2_b[:], row("b2"), row("ff_b2"), ALU.add).then_inc(setup_step, 1)
            pool.wait_ge(setup_step, 2)

            def residual_self(g):
                pool.wait_ge(z_ready["pre"], g + 1)
                if follows(g):
                    pool.wait_ge(y_ready["S"], g)
                nc.gpsimd.tensor_tensor(res["S"][:], xn[:], pairs(row("sa_bo")), ALU.add).then_inc(res_ready["S"], 1)

            def residual(n, frm, gain, bias, g):
                pool.wait_ge(z_ready[frm], g + 1)
                if follows(g):
                    pool.wait_ge(y_ready[n], g)
                nc.gpsimd.tensor_tensor(res[n][:], z[frm][:], pairs(gain), ALU.mult).then_inc(res_step[n], 1)
                pool.wait_ge(res_step[n], g + 1)
                nc.gpsimd.tensor_tensor(res[n][:], res[n][:], pairs(bias), ALU.add).then_inc(res_ready[n], 1)

            def roots(n, g):
                if n in ("pre", "4"):
                    pool.wait_ge(var_ready[n], g + 1)
                    src, power = var[n][:], const[:, C_POW + PAIRS:C_END]
                else:
                    pool.wait_ge(mean_done[n], g + 1)
                    src, power = mv[n][:, :, 1], const[:, C_POW:C_POW + PAIRS]
                if follows(g):
                    pool.wait_ge(z_ready[n], g)
                nc.gpsimd.tensor_tensor(root[n][:], src, power, ALU.pow).then_inc(root_ready[n], 1)

            def layer_output(g):
                pool.wait_ge(xres_loaded, 16 * (g + 1))
                if follows(g):
                    pool.wait_ge(xnew_ready, g)
                nc.gpsimd.tensor_tensor(xb3[:], xres[:], pairs(row("b3")), ALU.add).then_inc(xb3_ready, 1)
                pool.wait_ge(z_ready["3"], g + 1)
                if follows(g):
                    pool.wait_ge(z_ready["4"], g)
                nc.gpsimd.tensor_tensor(xnew[:], z["3"][:], pairs(row("g3")), ALU.mult).then_inc(xz_step, 1)
                pool.wait_ge(xz_step, g + 1)
                pool.wait_ge(xb3_ready, g + 1)
                nc.gpsimd.tensor_tensor(xnew[:], xnew[:], xb3[:], ALU.add).then_inc(xnew_ready, 1)

            def conv_bias(g):
                pool.wait_ge(xnew_ready, g + 1)
                if follows(g):
                    pool.wait_ge(pass_ready, g)
                nc.gpsimd.tensor_tensor(xnc[:], xnew[:], pairs(row("conv_b")), ALU.add).then_inc(xnc_ready, 1)

            def weigh_hidden(g):
                pool.wait_ge(cw_ready, g + 1)
                for p in range(PAIRS):
                    pool.wait_ge(hid_ready[p], g + 1)
                    if follows(g):
                        pool.wait_ge(hidT_done, g)
                    nc.gpsimd.tensor_tensor(
                        hidc[:, p].rearrange("p (e i) -> p e i", e=EXP), hid[:, p].rearrange("p (e i) -> p e i", e=EXP),
                        cwh[:, p].rearrange("p (e i) -> p e i", i=1).broadcast_to([P, EXP, INNER]),
                        ALU.mult).then_inc(hidc_ready[p], 1)

            def add_passes(g):
                pool.wait_ge(pass_ready, g + 1)
                if follows(g):
                    pool.wait_ge(out_ready, g)
                nc.gpsimd.tensor_tensor(rest[:], pass_x[:], pass_r[:], ALU.add).then_inc(rest_ready, 1)

            def iteration(t):
                if live(t):
                    residual_self(t)
                if live(t - 1):
                    roots("S", t - 1)
                if live(t - 3):
                    roots("3", t - 3)
                    layer_output(t - 3)
                if live(t + 1):
                    roots("pre", t + 1)
                if live(t - 3):
                    roots("4", t - 3)
                if live(t - 2):
                    roots("C", t - 2)
                if live(t - 1):
                    residual("C", "S", row("g1"), res1_b[:], t - 1)
                if live(t - 3):
                    conv_bias(t - 3)
                if live(t - 2):
                    residual("3", "C", row("g2"), res2_b[:], t - 2)
                if live(t - 3):
                    weigh_hidden(t - 3)
                if live(t - 3):
                    add_passes(t - 3)

            run(pool, iteration)

        @block.vector
        def _(dve):
            def chain(s, g, n):
                at = [0]

                def link(ins):
                    at[0] += 1
                    assert at[0] <= n
                    ins.then_inc(s, 1)
                    dve.wait_ge(s, g * n + at[0])
                return link

            dve.wait_ge(small_loaded, 96)
            nc.vector.tensor_scalar(bqs[:, 0:1], col("sa_bq"), SCALE, None, ALU.mult)
            nc.vector.tensor_scalar(bqs[:, 1:2], col("ca_bq"), SCALE, None, ALU.mult)
            nc.vector.tensor_scalar(bkh["S"][:], headmask, col("sa_bk"), None, ALU.mult)
            nc.vector.tensor_scalar(bkh["C"][:], headmask, col("ca_bk"), None, ALU.mult)
            nc.vector.tensor_scalar(neg_s[:], msk_s[:], 0.0, NEG, ALU.is_equal, ALU.mult)
            nc.vector.tensor_scalar(neg_c[:], msk_c[:], 0.0, NEG, ALU.is_equal, ALU.mult)
            for b in range(2):
                nc.vector.tensor_copy(pick_s[:, b * SEQ:(b + 1) * SEQ], const[0:SEQ, 0:SEQ])
            nc.vector.tensor_copy(pick_c[:], const[0:2, C_PAIR:C_PAIR + P])
            for k in range(TAPS):
                last = nc.vector.tensor_scalar(diag[:, k, :], ident, col(f"tap{k}"), None, ALU.mult)
            last.then_inc(dve_setup, 1)

            def soften(t, c):
                ph, g, r = slot(t, c)
                if not live(g):
                    return
                b, back = parity(c), two_back(ph, g, r)
                sc = S_BANK[b][:].rearrange("p (h k) -> p h k", k=SEQ)
                dve.wait_ge(scores_done[ph], ROWS * g + r + 1)
                nc.vector.tensor_reduce(out=rowmax[:, b, :], in_=sc, op=ALU.max, axis=AX_X).then_inc(max_done[ph], 1)
                dve.wait_ge(max_done[ph], ROWS * g + r + 1)
                if back:
                    dve.wait_ge(probT_done[back[0]], back[1])
                nc.vector.tensor_tensor(
                    prob[:, b, :].rearrange("p (h k) -> p h k", k=SEQ), sc,
                    rowmax[:, b, :].rearrange("p (h k) -> p h k", k=1).broadcast_to([P, 8, SEQ]),
                    ALU.subtract).then_inc(shift_done[ph], 1)

            def moments(n, src, g):
                for p in range(PAIRS):
                    last = nc.vector.bn_stats(stats[n][:, p, :], src[:, p, :])
                unit = 16 if n == "pre" else 1
                last.then_inc(stats_done[n], unit)
                settle(dve)
                dve.wait_ge(stats_done[n], unit * (g + 1))
                for p in range(PAIRS):
                    last = nc.vector.bn_aggr(mv[n][:, p, :], stats[n][:, p, :])
                last.then_inc(mean_done[n], 1)
                if n in ("pre", "4"):
                    dve.wait_ge(mean_done[n], g + 1)
                    nc.vector.tensor_scalar(var[n][:], mv[n][:, :, 1], EPS, None, ALU.add).then_inc(var_ready[n], 1)

            def normalise(n, src, dst, g, used, times=1):
                dve.wait_ge(root_ready[n], g + 1)
                scale = root[n]
                if n not in ("pre", "4"):
                    link = chain(inv_step[n], g, 2)
                    link(nc.vector.tensor_scalar(inv[n][:], root[n][:], EPS, None, ALU.add))
                    link(nc.vector.reciprocal(inv[n][:], inv[n][:]))
                    scale = inv[n]
                for s in used:
                    if follows(g):
                        dve.wait_ge(s, g)
                for p in range(PAIRS):
                    last = nc.vector.tensor_scalar(dst[:, p, :], src[:, p, :], mv[n][:, p, 0:1], scale[:, p:p + 1],
                                                   ALU.subtract, ALU.mult)
                last.then_inc(z_ready[n], 1)

            def post_moments(n, psum, g):
                dve.wait_ge(y_done[n], g + 1)
                dve.wait_ge(res_ready[n], g + 1)
                nc.vector.tensor_tensor(y[n][:].rearrange("p a m -> p (a m)"), psum[:, 0:TOK],
                                        res[n][:].rearrange("p a m -> p (a m)"), ALU.add).then_inc(y_ready[n], 1)
                dve.wait_ge(y_ready[n], g + 1)
                moments(n, y[n], g)

            def heads_out(ph, g):
                o = O_BANK[:, 0:2 * HEADS * VW].rearrange("p (h c) -> p h c", c=VW)
                dve.wait_ge(pv_done[ph], ROWS * (g + 1))
                nc.vector.reciprocal(rsum[ph][:], o[:, :, DK]).then_inc(osum_step[ph], 1)
                dve.wait_ge(osum_step[ph], g + 1)
                if follows(g):
                    dve.wait_ge(oT_done[ph], g)
                nc.vector.tensor_tensor(
                    o_tm[ph][:].rearrange("p a (h d) -> p (a h) d", d=DK), o[:, :, 0:DK],
                    rsum[ph][:].rearrange("p (h d) -> p h d", d=1).broadcast_to([P, 2 * HEADS, DK]),
                    ALU.mult).then_inc(o_ready[ph], 1)

            def route(g):
                link = chain(route_step, g, 10)
                dve.wait_ge(er_ready, g + 1)
                if follows(g):
                    dve.wait_ge(pass_ready, g)
                link(nc.vector.tensor_scalar(score[:], e_r[:], 1.0, None, ALU.add))
                link(nc.vector.reciprocal(score[:], score[:]))
                nc.vector.tensor_tensor(biased[:], score[:], pairs(rb[:]), ALU.add).then_inc(biased_done, 1)
                settle(dve)
                dve.wait_ge(biased_done, g + 1)
                for p in range(PAIRS):
                    last = nc.vector.max(top[:, p, :], biased[:, p, :])
                last.then_inc(top_done, 1)
                settle(dve)
                dve.wait_ge(top_done, g + 1)
                for p in range(PAIRS):
                    last = nc.vector.max_index(topi[:, p, :], top[:, p, :], biased[:, p, :])
                last.then_inc(topi_done, 1)
                dve.wait_ge(topi_done, g + 1)
                link(nc.vector.tensor_copy(topf[:], topi[:, :, 0:2]))
                for k, pk in enumerate((pick0, pick1)):
                    last = nc.vector.tensor_tensor(pk[:], pairs(iota8), topf[:, :, k:k + 1].broadcast_to([P, PAIRS, NE]),
                                                   ALU.is_equal)
                link(last)
                link(nc.vector.tensor_tensor(pick0[:], pick0[:], pick1[:], ALU.add))
                link(nc.vector.tensor_tensor(chosen[:], pick0[:], score[:], ALU.mult))
                link(nc.vector.tensor_reduce(out=wsum[:], in_=chosen[:], op=ALU.add, axis=AX_X))
                link(nc.vector.tensor_scalar(wsum[:], wsum[:], 1e-9, None, ALU.add))
                link(nc.vector.reciprocal(wsum[:], wsum[:]))
                if follows(g):
                    dve.wait_ge(hidc_ready[PAIRS - 1], g)
                link(nc.vector.tensor_tensor(
                    cw[:], chosen[:], wsum[:].rearrange("p (a m) -> p a m", m=1).broadcast_to([P, PAIRS, NE]), ALU.mult))
                nc.vector.tensor_scalar(cwh[:], cw[:, :, 0:EXP], 0.5, None, ALU.mult)
                nc.vector.tensor_tensor(c46[:], cw[:, :, EXP], cw[:, :, EXP + 2], ALU.add).then_inc(cw_ready, 1)

            def gate(g, p, psum):
                dve.wait_ge(th_ready[p], g + 1)
                nc.vector.scalar_tensor_tensor(out=sig[:, p], in0=th[:, p], scalar=1.0, in1=psum[:, 0:TOK],
                                               op0=ALU.add, op1=ALU.mult).then_inc(gate_step[p], 1)
                dve.wait_ge(gate_step[p], g + 1)
                if follows(g):
                    dve.wait_ge(hidc_ready[p], g)
                nc.vector.tensor_tensor(hid[:, p], psum[:, TOK:2 * TOK], sig[:, p], ALU.mult).then_inc(hid_ready[p], 1)

            def passes(g):
                dve.wait_ge(xnc_ready, g + 1)
                dve.wait_ge(cw_ready, g + 1)
                if follows(g):
                    dve.wait_ge(rest_ready, g)
                for p in range(PAIRS):
                    nc.vector.scalar_tensor_tensor(out=pass_x[:, p], in0=z["4"][:, p], scalar=c46[:, p:p + 1],
                                                   in1=xnc[:, p], op0=ALU.mult, op1=ALU.add)
                    last = nc.vector.tensor_scalar(pass_r[:, p], z["4"][:, p], 0.0, cw[:, p, EXP + 3:EXP + 4],
                                                   ALU.max, ALU.mult)
                last.then_inc(pass_ready, 1)

            def finish(g):
                dve.wait_ge(acc_done, g + 1)
                dve.wait_ge(rest_ready, g + 1)
                if follows(g):
                    dve.wait_ge(stored, 16 * g)
                nc.vector.tensor_tensor(y_out[:].rearrange("p a m -> p (a m)"), FFB[:, 0:TOK],
                                        rest[:].rearrange("p a m -> p (a m)"), ALU.add).then_inc(out_ready, 1)

            def iteration(t):
                soften(t, 0)
                if live(t - 1):
                    post_moments("S", POST, t - 1)
                if live(t - 3):
                    post_moments("3", FFB, t - 3)
                soften(t, 1)
                if live(t - 1):
                    normalise("S", y["S"], z["S"], t - 1, (zT_done["S"], res_ready["C"]))
                if live(t - 3):
                    normalise("3", y["3"], z["3"], t - 3, (xnew_ready,))
                if live(t - 2):
                    heads_out("C", t - 2)
                if live(t - 4):
                    finish(t - 4)
                soften(t, 2)
                if live(t + 1):
                    dve.wait_ge(x_loaded, 16 * (t + 2))
                    moments("pre", x_tm, t + 1)
                if live(t - 3):
                    dve.wait_ge(xnew_ready, t - 2)
                    moments("4", xnew, t - 3)
                soften(t, 3)
                if live(t + 1):
                    normalise("pre", x_tm, xn, t + 1, (zT_done["pre"], res_ready["S"]))
                if live(t - 3):
                    normalise("4", xnew, z["4"], t - 3, (zT_done["4"], pass_ready))
                if live(t - 2):
                    post_moments("C", POST, t - 2)
                soften(t, 4)
                if live(t - 2):
                    normalise("C", y["C"], z["C"], t - 2, (zT_done["C"], res_ready["3"]))
                soften(t, 5)
                if live(t):
                    heads_out("S", t)
                if live(t - 3):
                    gate(t - 3, 1, PROJ)
                    gate(t - 3, 0, FFB)
                    route(t - 3)
                soften(t, 6)
                soften(t, 7)
                if live(t - 3):
                    passes(t - 3)

            run(dve, iteration)

        @block.scalar
        def _(act):
            nc.scalar.preload_act_table_set("exp_and_others")
            act.wait_ge(dve_setup, 1)
            act.wait_ge(pool_setup, 2)

            def exponentials(t, c):
                ph, g, r = slot(t, c)
                if not live(g):
                    return
                b, back = parity(c), two_back(ph, g, r)
                act.wait_ge(shift_done[ph], ROWS * g + r + 1)
                nc.scalar.activation(prob[:, b, :], prob[:, b, :], ACT.Exp).then_inc(exp_done[ph], 1)

            def copy_probT(t, c):
                ph, g, r = slot(t, c)
                if not live(g):
                    return
                b, back = parity(c), two_back(ph, g, r)
                act.wait_ge(probT_done[ph], ROWS * g + r + 1)
                if back:
                    act.wait_ge(pv_done[back[0]], back[1])
                nc.scalar.activation(probT[:, b, :], PT_BANK[b][:], ACT.Copy).then_inc(probT_copied[ph], 1)

            def queries_keys(ph, g):
                bias = bqs[:, 0:1] if ph == "S" else bqs[:, 1:2]
                act.wait_ge(qk_done[ph], g + 1)
                if follows(g):
                    act.wait_ge(scores_done[ph], ROWS * g)
                for r in range(ROWS):
                    rg = slice(32 * r, 32 * r + 32)
                    nc.scalar.activation(qz[ph][rg, r, :], PROJ[rg, 0:TOK], ACT.Identity, bias=bias[rg], scale=SCALE)
                for h in range(HR):
                    last = nc.scalar.activation(kbd[ph][:, h, :], PROJ[:, TOK:2 * TOK], ACT.Identity,
                                                bias=bkh[ph][:, h:h + 1], scale=headmask[:, h:h + 1])
                last.then_inc(kbd_ready[ph], 1)

            def values(ph, g):
                act.wait_ge(v_done[ph], g + 1)
                if follows(g):
                    act.wait_ge(pv_done[ph], ROWS * g)
                for h in range(2):
                    rng = slice(h * SEQ, (h + 1) * SEQ)
                    last = nc.scalar.activation(
                        vbd[ph][rng, :, :, h, 0:DK].rearrange("p b j d -> p (b j) d"),
                        PROJ[rng, 0:TOK].rearrange("p (b d) -> p b d", d=DK), ACT.Copy)
                last.then_inc(vbd_ready[ph], 1)

            def heads_fm(ph, g):
                act.wait_ge(oT_done[ph], g + 1)
                if follows(g):
                    act.wait_ge(y_done[ph], g)
                nc.scalar.activation(oT[ph][:], POST[:, 0:TOK], ACT.Identity,
                                     bias=col("sa_bv" if ph == "S" else "ca_bv")).then_inc(oT_ready[ph], 1)

            def to_fm(n, dst, g, used, gain=None, bias=None):
                act.wait_ge(zT_done[n], g + 1)
                for s in used:
                    if follows(g):
                        act.wait_ge(s, g)
                if gain is None:
                    nc.scalar.activation(dst[:], POST[:, 0:TOK], ACT.Copy).then_inc(zT_ready[n], 1)
                else:
                    nc.scalar.activation(dst[:], POST[:, 0:TOK], ACT.Identity, bias=col(bias),
                                         scale=col(gain)).then_inc(zT_ready[n], 1)

            def context_fm(g):
                act.wait_ge(encT_done, g + 1)
                if follows(g):
                    act.wait_ge(v_done["C"], g)
                nc.scalar.activation(encT[:], POST[:, 0:TOK], ACT.Copy).then_inc(encT_ready, 1)

            def hidden(half, g):
                act.wait_ge(h_done[half], g + 1)
                if follows(g):
                    act.wait_ge(y_done["3"], g)
                for c in range(2):
                    last = nc.scalar.activation(hT[:, 2 * half + c, :], FFB[:, c * TOK:(c + 1) * TOK], ACT.Relu,
                                                bias=col(f"ff{2 * half + c}"))
                last.then_inc(h_ready[half], 1)

            def mixture_fm(g):
                act.wait_ge(zT_done["4"], g + 1)
                if follows(g):
                    act.wait_ge(acc_done, g)
                nc.scalar.activation(z4T[:, :, TAPS - 1:], FFB[:, 0:TOK].rearrange("p (b s) -> p b s", b=BATCH),
                                     ACT.Copy).then_inc(zT_ready["4"], 1)

            def router_exp(g):
                act.wait_ge(logits_done, g + 1)
                if follows(g):
                    act.wait_ge(cw_ready, g)
                nc.scalar.activation(e_r[:].rearrange("p a m -> p (a m)"), FFB[:, 0:PAIRS * NE], ACT.Exp,
                                     scale=-1.0).then_inc(er_ready, 1)

            def gate_tanh(g, p, psum):
                act.wait_ge(gu_done[p], g + 1)
                if follows(g):
                    act.wait_ge(hid_ready[p], g)
                nc.scalar.activation(th[:, p], psum[:, 0:TOK], ACT.Tanh, scale=0.5).then_inc(th_ready[p], 1)

            def hidden_fm(g):
                act.wait_ge(hidT_done, g + 1)
                if follows(g):
                    act.wait_ge(acc_done, g)
                nc.scalar.activation(hidT[:].rearrange("p a c t -> p (a c t)"), PROJ[:], ACT.Copy).then_inc(hidT_ready, 1)

            def iteration(t):
                copy_probT(t, -1)
                exponentials(t, 0)
                if live(t - 1):
                    context_fm(t - 1)
                copy_probT(t, 0)
                exponentials(t, 1)
                if live(t - 1):
                    to_fm("S", src_fm["C"], t - 1, (qk_done["C"],), "g1", "b1")
                copy_probT(t, 1)
                exponentials(t, 2)
                if live(t - 1):
                    queries_keys("C", t - 1)
                if live(t - 2):
                    heads_fm("C", t - 2)
                copy_probT(t, 2)
                exponentials(t, 3)
                if live(t - 1):
                    values("C", t - 1)
                copy_probT(t, 3)
                exponentials(t, 4)
                if live(t - 3):
                    mixture_fm(t - 3)
                if live(t + 1):
                    to_fm("pre", src_fm["S"], t + 1, (v_done["S"],))
                copy_probT(t, 4)
                exponentials(t, 5)
                if live(t - 3):
                    router_exp(t - 3)
                    gate_tanh(t - 3, 1, PROJ)
                    gate_tanh(t - 3, 0, FFB)
                if live(t - 2):
                    to_fm("C", x2T, t - 2, (h_done[1],), "g2", "b2")
                copy_probT(t, 5)
                exponentials(t, 6)
                if live(t):
                    heads_fm("S", t)
                if live(t + 1):
                    queries_keys("S", t + 1)
                if live(t - 2):
                    hidden(0, t - 2)
                copy_probT(t, 6)
                exponentials(t, 7)
                if live(t + 1):
                    values("S", t + 1)
                if live(t - 2):
                    hidden(1, t - 2)
                if live(t - 3):
                    hidden_fm(t - 3)

            run(act, iteration)

        @block.tensor
        def _(pe):
            mm = nc.tensor.matmul
            pe.wait_ge(small_loaded, 96)
            pe.wait_ge(dve_setup, 1)

            def scores(t, c):
                ph, g, r = slot(t, c)
                if not live(g):
                    return
                s, back = S_BANK[parity(c)], two_back(ph, g, r)
                if ph == "C":
                    settle(pe)
                if back:
                    pe.wait_ge(shift_done[back[0]], back[1])
                if ph == "S":
                    mm(s[:].rearrange("p (h k) -> p h k", k=SEQ), pick_s[:],
                       neg_s[:].rearrange("p (h k) -> p h k", h=1).broadcast_to([SEQ, 8, SEQ]),
                       start=True, stop=False, skip_group_check=True)
                else:
                    for p in range(PAIRS):
                        mm(s[:, p * TOK:(p + 1) * TOK].rearrange("p (h k) -> p h k", k=SEQ), pick_c[:],
                           neg_c[:, g * PAIRS + p, :].rearrange("p (h k) -> p h k", h=1).broadcast_to([2, HR, SEQ])
                           if isinstance(g, int) else
                           neg_c[:, bass.ds(g * PAIRS + p, 1), :].broadcast_to([2, HR, SEQ]),
                           start=p == 0, stop=False, skip_group_check=True)
                if r == 0:
                    pe.wait_ge(kbd_ready[ph], g + 1)
                for p in range(PAIRS):
                    for b in range(2):
                        tok = slice(p * P + b * SEQ, p * P + (b + 1) * SEQ)
                        last = mm(s[b * SEQ:(b + 1) * SEQ, p * TOK:(p + 1) * TOK].rearrange("p (h k) -> p h k", k=SEQ),
                                  qz[ph][:, r, tok], kbd[ph][:, :, tok], start=False, stop=True, skip_group_check=True)
                last.then_inc(scores_done[ph], 1)

            def turn_probs(t, c):
                ph, g, r = slot(t, c)
                if not live(g):
                    return
                b, back = parity(c), two_back(ph, g, r)
                pe.wait_ge(exp_done[ph], ROWS * g + r + 1)
                if back:
                    pe.wait_ge(probT_copied[back[0]], back[1])
                for j in range(4):
                    last = nc.tensor.transpose(PT_BANK[b][:, j * P:(j + 1) * P], prob[:, b, j * P:(j + 1) * P], ident)
                last.then_inc(probT_done[ph], 1)

            def heads(t, c):
                ph, g, r = slot(t, c)
                if not live(g):
                    return
                b, back = parity(c), two_back(ph, g, r)
                if r == 0:
                    pe.wait_ge(vbd_ready[ph], g + 1)
                    other = ("C", g - 2) if ph == "S" else ("S", g + 1)
                    if live(other[1]):
                        pe.wait_ge(o_ready[other[0]], other[1] + 1)
                    else:
                        if follows(g):
                            pe.wait_ge(o_ready[ph], g)
                pe.wait_ge(probT_copied[ph], ROWS * g + r + 1)
                for p in range(PAIRS):
                    for jj in range(2):
                        for sq in range(2):
                            j = 2 * r + jj
                            o = (p * HEADS + 2 * j) * VW
                            last = mm(O_BANK[sq * SEQ:(sq + 1) * SEQ, o:o + 2 * VW],
                                      probT[:, b, (2 * p + jj) * P + sq * SEQ:(2 * p + jj) * P + (sq + 1) * SEQ],
                                      vbd[ph][:, 2 * p + sq, j].rearrange("p h c -> p (h c)"),
                                      start=True, stop=True)
                last.then_inc(pv_done[ph], 1)

            def attend(t, c):
                scores(t, c)
                turn_probs(t, c - 1)
                heads(t, c - 2)

            def transpose_pairs(dst, src, s):
                for p in range(PAIRS):
                    last = nc.tensor.transpose(dst[:, p * P:(p + 1) * P], src[:, p], ident)
                last.then_inc(s, 1)

            def project_qk(ph, g, t, use):
                if isinstance(t, int):
                    pe.wait_ge(proj_loaded, 128)
                read = last_read(PROJ_USES, use, t)
                if read:
                    pe.wait_ge(*read)
                pe.wait_ge(zT_ready["pre" if ph == "S" else "S"], g + 1)
                if ph == "C":
                    pe.wait_ge(encT_ready, g + 1)
                mm(PROJ[:, 0:TOK], w[ph]["q"][:], src_fm[ph][:], start=True, stop=True)
                mm(PROJ[:, TOK:2 * TOK], w[ph]["k"][:], kv_fm[ph][:], start=True, stop=True).then_inc(qk_done[ph], 1)

            def project_v(ph, g, t, use):
                read = last_read(PROJ_USES, use, t)
                if read:
                    pe.wait_ge(*read)
                wv = w[ph]["v"][:].rearrange("p (j h d) -> p h j d", h=2, d=DK)
                for b in range(BATCH):
                    for h in range(2):
                        last = mm(PROJ[h * SEQ:(h + 1) * SEQ, b * SEQ:(b + 1) * SEQ].rearrange("p (j d) -> p j d", d=DK),
                                  kv_fm[ph][:, b * SEQ:(b + 1) * SEQ], wv[:, h], start=True, stop=True)
                last.then_inc(v_done[ph], 1)

            def heads_to_fm(ph, g, t, use):
                read = last_read(POST_USES, use, t)
                if read:
                    pe.wait_ge(*read)
                pe.wait_ge(o_ready[ph], g + 1)
                transpose_pairs(POST, o_tm[ph], oT_done[ph])

            def output_product(ph, g, t, use):
                read = last_read(POST_USES, use, t)
                if read:
                    pe.wait_ge(*read)
                pe.wait_ge(oT_ready[ph], g + 1)
                for p in range(PAIRS):
                    last = mm(POST[:, p * P:(p + 1) * P], oT[ph][:, p * P:(p + 1) * P], w[ph]["o"][:],
                              start=True, stop=True)
                last.then_inc(y_done[ph], 1)

            def z_to_fm(n, src, dst, uses, g, t, use):
                read = last_read(uses, use, t)
                if read:
                    pe.wait_ge(*read)
                pe.wait_ge(z_ready[n], g + 1)
                transpose_pairs(dst, src, zT_done[n])

            def context_to_fm(g, t, use):
                read = last_read(POST_USES, use, t)
                if read:
                    pe.wait_ge(*read)
                pe.wait_ge(ctx_loaded, 16 * (g + 1))
                transpose_pairs(POST, ctx_tm, encT_done)

            def ffn_in(half, g, t, use):
                if isinstance(t, int):
                    pe.wait_ge(ffn_loaded, 32)
                read = last_read(FFB_USES, use, t)
                if read:
                    pe.wait_ge(*read)
                pe.wait_ge(zT_ready["C"], g + 1)
                for c in range(2):
                    k = 2 * half + c
                    last = mm(FFB[:, c * TOK:(c + 1) * TOK], w1_sb[:, k * P:(k + 1) * P], x2T[:], start=True, stop=True)
                last.then_inc(h_done[half], 1)

            def ffn_out(g, t, use):
                read = last_read(FFB_USES, use, t)
                if read:
                    pe.wait_ge(*read)
                pe.wait_ge(h_ready[1], g + 1)
                for p in range(PAIRS):
                    for k in range(FF):
                        last = mm(FFB[:, p * P:(p + 1) * P], hT[:, k, p * P:(p + 1) * P], w2_sb[:, k, :],
                                  start=k == 0, stop=k == FF - 1)
                last.then_inc(y_done["3"], 1)

            def tokens4(p, b, k):
                return z4T[:, 2 * p + b, k:k + SEQ]

            def logits(g, t, use):
                if isinstance(t, int):
                    pe.wait_ge(mix_loaded, 64)
                read = last_read(FFB_USES, use, t)
                if read:
                    pe.wait_ge(*read)
                pe.wait_ge(zT_ready["4"], g + 1)
                for p in range(PAIRS):
                    for b in range(2):
                        last = mm(FFB[b * SEQ:(b + 1) * SEQ, p * NE:(p + 1) * NE], tokens4(p, b, TAPS - 1), wr_sb[:],
                                  start=True, stop=True)
                last.then_inc(logits_done, 1)

            def gate_up(p, dst, uses, g, t, use):
                read = last_read(uses, use, t)
                if read:
                    pe.wait_ge(*read)
                for b in range(2):
                    last = mm(dst[b * SEQ:(b + 1) * SEQ, :], tokens4(p, b, TAPS - 1),
                              wgu_sb[:].rearrange("p a e i -> p (a e i)"), start=True, stop=True)
                last.then_inc(gu_done[p], 1)

            def hidden_to_fm(g, t, use):
                read = last_read(PROJ_USES, use, t)
                if read:
                    pe.wait_ge(*read)
                for p in range(PAIRS):
                    pe.wait_ge(hidc_ready[p], g + 1)
                    for c in range(2):
                        last = nc.tensor.transpose(PROJ[:, (2 * p + c) * P:(2 * p + c + 1) * P],
                                                   hidc[:, p, c * P:(c + 1) * P], ident)
                last.then_inc(hidT_done, 1)

            def mix(g, t, use):
                read = last_read(FFB_USES, use, t)
                if read:
                    pe.wait_ge(*read)
                pe.wait_ge(hidT_ready, g + 1)
                for p in range(PAIRS):
                    tok = slice(p * P, (p + 1) * P)
                    for b in range(2):
                        for k in range(TAPS):
                            mm(FFB[b * SEQ:(b + 1) * SEQ, tok], tokens4(p, b, k), diag[:, k, :],
                               start=k == 0, stop=False, skip_group_check=True)
                    for c in range(2):
                        last = mm(FFB[:, tok], hidT[:, p, c, :], wd_sb[:, c, :], start=False, stop=c == 1,
                                  skip_group_check=True)
                last.then_inc(acc_done, 1)

            def iteration(t):
                attend(t, 0)
                if live(t - 3):
                    ffn_out(t - 3, t, 0)
                if live(t - 1):
                    context_to_fm(t - 1, t, 0)
                attend(t, 1)
                if live(t - 4):
                    mix(t - 4, t, 1)
                if live(t - 1):
                    z_to_fm("S", z["S"], POST, POST_USES, t - 1, t, 1)
                attend(t, 2)
                if live(t - 1):
                    project_qk("C", t - 1, t, 0)
                if live(t - 2):
                    heads_to_fm("C", t - 2, t, 2)
                attend(t, 3)
                if live(t - 1):
                    project_v("C", t - 1, t, 1)
                if live(t - 2):
                    output_product("C", t - 2, t, 3)
                attend(t, 4)
                if live(t - 3):
                    z_to_fm("4", z["4"], FFB, FFB_USES, t - 3, t, 2)
                if live(t + 1):
                    z_to_fm("pre", xn, POST, POST_USES, t + 1, t, 4)
                attend(t, 5)
                if live(t - 3):
                    logits(t - 3, t, 3)
                    gate_up(1, PROJ, PROJ_USES, t - 3, t, 2)
                    gate_up(0, FFB, FFB_USES, t - 3, t, 4)
                if live(t - 2):
                    z_to_fm("C", z["C"], POST, POST_USES, t - 2, t, 5)
                attend(t, 6)
                if live(t):
                    heads_to_fm("S", t, t, 6)
                if live(t + 1):
                    project_qk("S", t + 1, t, 3)
                if live(t - 2):
                    ffn_in(0, t - 2, t, 5)
                attend(t, 7)
                if live(t + 1):
                    project_v("S", t + 1, t, 4)
                if live(t):
                    output_product("S", t, t, 7)
                if live(t - 2):
                    ffn_in(1, t - 2, t, 6)
                if live(t - 3):
                    hidden_to_fm(t - 3, t, 5)

            run(pe, iteration)


def constants():
    import numpy as np

    c = np.zeros((P, C_END), np.float32)
    c[:, C_ID:C_ID + P] = np.eye(P)
    for p in range(P):
        c[p, C_HEAD + p % 32 // DK] = 1
    c[:, C_IOTA:C_IOTA + NE] = np.arange(NE)
    for b in range(2):
        c[b, C_PAIR + b * SEQ:C_PAIR + (b + 1) * SEQ] = 1
    c[:, C_POW:C_POW + PAIRS] = 0.5
    c[:, C_POW + PAIRS:C_END] = -0.5
    return c


def kernel(**inputs):
    import numpy as np
    import concourse.bacc as bacc
    from concourse.bass_utils import run_bass_kernel_spmd

    i = {k.replace("L0_xattn_", "").replace("L0_ffn_", ""): np.asarray(v) for k, v in inputs.items()}
    ff = i["ff_b1"].reshape(FF, P)
    taps = i["conv_w"].reshape(TAPS, P)
    per_partition = [i[n] for n in COLS[:10]] + [ff[k] for k in range(FF)] + [taps[k] for k in range(TAPS)]
    per_feature = [i[n] for n in ROWV]
    arrays = {
        "x": i["x"], "ctx": i["ctx_1024"], "mask_self": i["mask_SxS2_ik0"], "mask_cross": i["mask_Bx1x1xS2_if1"],
        "wq_s": i["sa_wq"], "wk_s": i["sa_wk"], "wv_s": i["sa_wv"], "wo_s": i["sa_wo"],
        "wq_c": i["ca_wq"], "wk_c": i["ca_wk"], "wv_c": i["ca_wv"], "wo_c": i["ca_wo"],
        "w1": i["ff_w1"], "w2": i["ff_w2"], "wr": i["Wr"], "wg": i["Wg"], "wu": i["Wu"], "wd": i["Wd"],
        "cols_d": np.stack(per_partition, axis=1), "rows_d": np.concatenate(per_feature)[None, :],
        "rb_d": i["router_bias"][None, :], "const_d": constants(),
    }
    nc = bacc.Bacc("TRN2", target_bir_lowering=False, num_devices=1)
    args = {}
    for name, a in arrays.items():
        arrays[name] = a = np.ascontiguousarray(a)
        args[name] = nc.dram_tensor(name, a.shape, mybir.dt.from_np(a.dtype), kind="ExternalInput").ap()
    args["out"] = nc.dram_tensor("out", i["x"].shape, F32, kind="ExternalOutput").ap()
    program(nc, **args)
    r = run_bass_kernel_spmd(nc, [arrays], core_ids=[0])
    return r.results[0]["out"]
```

```python
from contextlib import ExitStack

import concourse.bass as bass
from concourse import mybir

F32 = mybir.dt.float32
BF16 = mybir.dt.bfloat16
I32 = mybir.dt.int32
U32 = mybir.dt.uint32
ALU = mybir.AluOpType
ACT = mybir.ActivationFunctionType
AX_X = mybir.AxisListType.X

P = 128
SEQ = 64
HEADS, DK = 16, 8
PAIRS = 2
TOK = PAIRS * P
BATCH = TOK // SEQ
ROWS = 4
HR = HEADS // ROWS
FF = 4
EXP, INNER = 4, 64
NE = 8
TAPS = 4
VW = DK + 1
NEG = -float(2 ** 100)
EPS = 1e-5

COLS = ["sa_bq", "sa_bk", "sa_bv", "ca_bq", "ca_bk", "ca_bv", "g1", "b1", "g2", "b2",
        "ff0", "ff1", "ff2", "ff3", "tap0", "tap1", "tap2", "tap3"]
ROWV = ["sa_bo", "g1", "b1", "ca_bo", "g2", "b2", "ff_b2", "g3", "b3", "conv_b"]
C_ID, C_HEAD, C_IOTA, C_PAIR, C_POW = 0, P, P + HR, P + HR + NE, P + HR + NE + P
C_END = C_POW + 2 * PAIRS


def program(nc, x, ctx, mask_self, mask_cross, wq_s, wk_s, wv_s, wo_s, wq_c, wk_c, wv_c, wo_c,
            w1, w2, wr, wg, wu, wd, cols_d, rows_d, rb_d, const_d, out):
    GROUPS = x.shape[0] * SEQ // TOK
    SCALE = float(DK) ** -0.5

    def by_group(a):
        return a.rearrange("b s d -> (b s) d").rearrange("(g p t) d -> g t p d", p=PAIRS, t=P)

    x_g, ctx_g, out_g = by_group(x), by_group(ctx), by_group(out)

    with ExitStack() as stack:
        def sb(name, shape, dt=F32):
            return stack.enter_context(nc.sbuf_tensor(name, shape, dt))

        def sem(name):
            return stack.enter_context(nc.semaphore(name))

        bank = [stack.enter_context(nc.psum_tensor(f"bank{i}", [P, 512], F32)) for i in range(8)]
        S_BANK, PT_BANK = bank[0:2], bank[2:4]
        O_BANK, PROJ, POST, FFB = bank[4:8]
        POST2 = POST[:, TOK:2 * TOK]

        w = {"S": {}, "C": {}}
        for ph in "SC":
            for n in ("q", "k", "v", "o"):
                w[ph][n] = sb(f"w{n}_{ph}", [P, P])
        w1_sb = sb("w1_sb", [P, FF * P])
        w2_sb = sb("w2_sb", [P, FF, P])
        wr_sb = sb("wr_sb", [P, NE])
        wgu_sb = sb("wgu_sb", [P, 2, EXP, INNER])
        wd_sb = sb("wd_sb", [P, 2, P])
        cols = sb("cols", [P, len(COLS)])
        rows = sb("rows", [P, len(ROWV), P])
        rb = sb("rb", [P, NE])
        const = sb("const", [P, C_END])
        msk_s = sb("msk_s", [SEQ, SEQ], I32)
        msk_c = sb("msk_c", [2, GROUPS * PAIRS, SEQ], I32)
        neg_s = sb("neg_s", [SEQ, SEQ], BF16)
        neg_c = sb("neg_c", [2, GROUPS * PAIRS, SEQ], BF16)
        pick_s = sb("pick_s", [SEQ, P], BF16)
        pick_c = sb("pick_c", [2, P], BF16)
        bqs = sb("bqs", [P, 2])
        diag = sb("diag", [P, TAPS, P])
        res1_b = sb("res1_b", [P, P])
        res2_b = sb("res2_b", [P, P])
        ident = const[:, C_ID:C_ID + P]
        headmask = const[:, C_HEAD:C_HEAD + HR]
        iota8 = const[:, C_IOTA:C_IOTA + NE]

        def col(name):
            return cols[:, COLS.index(name):COLS.index(name) + 1]

        def row(name):
            return rows[:, ROWV.index(name), :]

        def pairs(r, n=PAIRS):
            return r.rearrange("p (a m) -> p a m", a=1).broadcast_to([P, n, r.shape[1]])

        x_tm = sb("x_tm", [P, PAIRS, P])
        ctx_tm = sb("ctx_tm", [P, PAIRS, P])
        xres = sb("xres", [P, PAIRS, P])
        xn = sb("xn", [P, PAIRS, P])
        src_fm = {"S": sb("xnT", [P, TOK]), "C": sb("x1T", [P, TOK])}
        encT = sb("encT", [P, TOK])
        kv_fm = {"S": src_fm["S"], "C": encT}
        x2T = sb("x2T", [P, TOK])
        qz = {ph: sb(f"qz_{ph}", [P, ROWS, TOK]) for ph in "SC"}
        kT = {ph: sb(f"kT_{ph}", [P, TOK]) for ph in "SC"}
        kbd = {ph: sb(f"kbd_{ph}", [P, HR, TOK]) for ph in "SC"}
        vbd = {ph: sb(f"vbd_{ph}", [P, BATCH, HEADS // 2, 2, VW]) for ph in "SC"}
        rowmax = sb("rowmax", [P, 2, 8])
        prob = sb("prob", [P, 2, 512])
        probT = sb("probT", [P, 2, 512])
        rsum = {ph: sb(f"rsum_{ph}", [P, 2 * HEADS]) for ph in "SC"}
        o_tm = {ph: sb(f"o_tm_{ph}", [P, PAIRS, P]) for ph in "SC"}
        oT = {ph: sb(f"oT_{ph}", [P, TOK]) for ph in "SC"}
        LN = ("pre", "S", "C", "3", "4")
        y = {n: sb(f"y_{n}", [P, PAIRS, P]) for n in ("S", "C", "3")}
        z = {n: sb(f"z_{n}", [P, PAIRS, P]) for n in ("S", "C", "3", "4")}
        res = {n: sb(f"res_{n}", [P, PAIRS, P]) for n in ("S", "C", "3")}
        stats = {n: sb(f"stats_{n}", [P, PAIRS, 6]) for n in LN}
        mv = {n: sb(f"mv_{n}", [P, PAIRS, 2]) for n in LN}
        var = {n: sb(f"var_{n}", [P, PAIRS]) for n in LN}
        root = {n: sb(f"root_{n}", [P, PAIRS]) for n in LN}
        inv = {n: sb(f"inv_{n}", [P, PAIRS]) for n in LN}
        hT = sb("hT", [P, FF, TOK])
        xb3 = sb("xb3", [P, PAIRS, P])
        xnew = sb("xnew", [P, PAIRS, P])
        xnc = sb("xnc", [P, PAIRS, P])
        z4T = sb("z4T", [P, BATCH, TAPS - 1 + SEQ])
        e_r = sb("e_r", [P, PAIRS, NE])
        score = sb("score", [P, PAIRS, NE])
        biased = sb("biased", [P, PAIRS, NE])
        top = sb("top", [P, PAIRS, 8])
        topi = sb("topi", [P, PAIRS, 8], U32)
        topf = sb("topf", [P, PAIRS, 2])
        pick0 = sb("pick0", [P, PAIRS, NE])
        pick1 = sb("pick1", [P, PAIRS, NE])
        chosen = sb("chosen", [P, PAIRS, NE])
        wsum = sb("wsum", [P, PAIRS])
        cw = sb("cw", [P, PAIRS, NE])
        cwh = sb("cwh", [P, PAIRS, EXP])
        c46 = sb("c46", [P, PAIRS])
        th = sb("th", [P, PAIRS, EXP * INNER])
        sig = sb("sig", [P, PAIRS, EXP * INNER])
        hid = sb("hid", [P, PAIRS, EXP * INNER])
        hidc = sb("hidc", [P, PAIRS, EXP * INNER])
        hidT = sb("hidT", [P, PAIRS, 2, P])
        pass_x = sb("pass_x", [P, PAIRS, P])
        pass_r = sb("pass_r", [P, PAIRS, P])
        rest = sb("rest", [P, PAIRS, P])
        y_out = sb("y_out", [P, PAIRS, P])

        first_loaded, mask_loaded, rows_loaded = sem("first_loaded"), sem("mask_loaded"), sem("rows_loaded")
        ffn_loaded, mix_loaded = sem("ffn_loaded"), sem("mix_loaded")
        x_loaded, ctx_loaded, xres_loaded, stored = (sem(n) for n in
                                                     ("x_loaded", "ctx_loaded", "xres_loaded", "stored"))
        dve_setup, pool_setup, setup_step = sem("dve_setup"), sem("pool_setup"), sem("setup_step")

        def both(name):
            return {ph: sem(f"{name}_{ph}") for ph in "SC"}

        proj_loaded = both("proj_loaded")
        scores_done, max_done, shift_done, exp_done = (both(n) for n in ("scores", "max", "shift", "exp"))
        probT_done, probT_copied, pv_done = (both(n) for n in ("probT", "probTc", "pv"))
        qk_done, v_done, q_ready = (both(n) for n in ("qk", "v", "q"))
        kT_ready, kbd_ready, vbd_ready = (both(n) for n in ("kT", "kbd", "vbd"))
        osum_step, o_ready, oT_done, oT_ready = (both(n) for n in ("osum", "o", "oTps", "oT"))
        y_done = {n: sem(f"yps_{n}") for n in ("S", "C", "3")}
        y_ready = {n: sem(f"y_{n}r") for n in ("S", "C", "3")}
        res_step = {n: sem(f"res_step_{n}") for n in ("S", "C", "3")}
        res_ready = {n: sem(f"res_{n}r") for n in ("S", "C", "3")}
        stats_done = {n: sem(f"stats_{n}d") for n in LN}
        mean_done = {n: sem(f"mean_{n}d") for n in LN}
        var_ready = {n: sem(f"var_{n}r") for n in LN}
        root_ready = {n: sem(f"root_{n}r") for n in LN}
        inv_step = {n: sem(f"inv_step_{n}") for n in LN}
        z_ready = {n: sem(f"z_{n}r") for n in LN}
        zT_done = {n: sem(f"zTps_{n}") for n in LN}
        zT_ready = {n: sem(f"zT_{n}r") for n in LN}
        encT_done, encT_ready = sem("encTps"), sem("encT_ready")
        h_done = [sem("h_ps0"), sem("h_ps1")]
        h_ready = [sem("h_ready0"), sem("h_ready1")]
        xb3_ready, xz_step, xnew_ready, xnc_ready = (sem(n) for n in ("xb3", "xz_step", "xnew_r", "xnc_r"))
        logits_done, er_ready, route_step, cw_ready = (sem(n) for n in ("logits", "er", "route_step", "cw"))
        biased_done, top_done, topi_done = sem("biased_d"), sem("top_d"), sem("topi_d")
        gu_done = [sem("gu_ps0"), sem("gu_ps1")]
        th_ready = [sem("th0"), sem("th1")]
        gate_step = [sem("gate_step0"), sem("gate_step1")]
        hid_ready = [sem("hid0"), sem("hid1")]
        hidc_ready = [sem("hidc0"), sem("hidc1")]
        hidT_done, hidT_ready, acc_done = sem("hidTps"), sem("hidT_ready"), sem("acc")
        pass_ready, rest_ready, out_ready = sem("pass_r_sem"), sem("rest_sem"), sem("out_sem")

        def live(g):
            return not isinstance(g, int) or 0 <= g < GROUPS

        def follows(g):
            return not isinstance(g, int) or g >= 1

        def slot(t, c):
            if c < 0:
                t, c = t - 1, c + 2 * ROWS
            return ("S", t, c) if c < ROWS else ("C", t - 1, c - ROWS)

        def two_back(ph, g, r):
            if r >= 2:
                return ph, ROWS * g + r - 1
            other, og = ("C", g - 2) if ph == "S" else ("S", g + 1)
            if not live(og):
                other, og = ph, g - 1
            return (other, ROWS * og + r + 3) if live(og) else None

        def parity(r):
            return r % 2

        PROJ_USES = [(q_ready["C"], -1), (hidT_ready, -4), (hid_ready[1], -3), (q_ready["S"], 1)]
        POST_USES = [(zT_ready["S"], -1), (encT_ready, -1), (oT_ready["C"], -2), (vbd_ready["C"], -1),
                     (y_ready["C"], -2), (zT_ready["pre"], 1), (zT_ready["4"], -3), (zT_ready["C"], -2),
                     (oT_ready["S"], 0), (vbd_ready["S"], 1), (y_ready["S"], 0)]
        FFB_USES = [(y_ready["3"], -3), (out_ready, -4), (er_ready, -3), (hid_ready[0], -3), (h_ready[0], -2),
                    (h_ready[1], -2)]

        def last_read(uses, n, t):
            for back in range(1, len(uses) + 1):
                m = n - back
                s, off = uses[m % len(uses)]
                g = t + off - (1 if m < 0 else 0)
                if live(g):
                    return s, g + 1
            return None

        def settle(eng):
            eng.wait_ge(first_loaded, 32)

        block = stack.enter_context(nc.Block())

        def run(eng, iteration):
            first, last = 4, GROUPS - 2
            for t in range(-1, first):
                iteration(t)
            with eng.Fori(first, last) as t:
                iteration(t)
            for t in range(last, GROUPS + 4):
                iteration(t)

        @block.sync
        def _(sp):
            def load_x(g):
                if follows(g):
                    sp.wait_ge(z_ready["pre"], g)
                sp.dma_start(x_tm[:], x_g[g]).then_inc(x_loaded, 16)

            def load_ctx(g):
                if follows(g):
                    sp.wait_ge(encT_done, g)
                sp.dma_start(ctx_tm[:], ctx_g[g]).then_inc(ctx_loaded, 16)

            def load_xres(g):
                if follows(g):
                    sp.wait_ge(xb3_ready, g)
                sp.dma_start(xres[:], x_g[g]).then_inc(xres_loaded, 16)

            load_x(0)
            sp.dma_start(cols[:], cols_d).then_inc(first_loaded, 16)
            for n, a in (("k", wk_s), ("o", wo_s)):
                sp.dma_start(w["S"][n][:], a).then_inc(proj_loaded["S"], 16)
            sp.dma_start(msk_c[:], mask_cross.rearrange("(t b) i j k -> b t (i j k)", b=2)).then_inc(mask_loaded, 16)
            sp.dma_start(rb[:], rb_d.broadcast_to([P, NE])).then_inc(rows_loaded, 16)
            load_x(1)
            for n, a in (("q", wq_c), ("k", wk_c), ("v", wv_c), ("o", wo_c)):
                sp.dma_start(w["C"][n][:], a).then_inc(proj_loaded["C"], 16)

            def iteration(t):
                if live(t):
                    load_ctx(t)
                if live(t - 2):
                    load_xres(t - 2)
                if live(t - 4):
                    sp.wait_ge(out_ready, t - 3)
                    sp.dma_start(out_g[t - 4], y_out[:]).then_inc(stored, 16)
                if live(t + 2) and not (isinstance(t, int) and t < 0):
                    load_x(t + 2)

            run(sp, iteration)
            sp.wait_ge(stored, 16 * GROUPS)

        @block.gpsimd
        def _(pool):
            def clear(ph, zeros, step):
                for buf in zeros:
                    last = nc.gpsimd.memset(buf[:], 0.0)
                last.then_inc(setup_step, 1)
                pool.wait_ge(setup_step, step)
                nc.gpsimd.memset(vbd[ph][0:SEQ, :, :, 0, DK:VW], 1.0)
                nc.gpsimd.memset(vbd[ph][SEQ:P, :, :, 1, DK:VW], 1.0).then_inc(pool_setup, 1)

            def late_setup():
                clear("C", (qz["C"], vbd["C"], z4T), 2)
                pool.wait_ge(pool_setup, 2)
                pool.wait_ge(rows_loaded, 32)
                nc.gpsimd.tensor_tensor(res1_b[:], row("b1"), row("ca_bo"), ALU.add)
                nc.gpsimd.tensor_tensor(res2_b[:], row("b2"), row("ff_b2"), ALU.add).then_inc(setup_step, 1)
                pool.wait_ge(setup_step, 3)

            clear("S", (qz["S"], vbd["S"]), 1)
            pool.wait_ge(pool_setup, 1)
            pool.wait_ge(first_loaded, 32)

            def residual_self(g):
                pool.wait_ge(z_ready["pre"], g + 1)
                if follows(g):
                    pool.wait_ge(y_ready["S"], g)
                nc.gpsimd.tensor_tensor(res["S"][:], xn[:], pairs(row("sa_bo")), ALU.add).then_inc(res_ready["S"], 1)

            def residual(n, frm, gain, bias, g):
                pool.wait_ge(z_ready[frm], g + 1)
                if follows(g):
                    pool.wait_ge(y_ready[n], g)
                nc.gpsimd.tensor_tensor(res[n][:], z[frm][:], pairs(gain), ALU.mult).then_inc(res_step[n], 1)
                pool.wait_ge(res_step[n], g + 1)
                nc.gpsimd.tensor_tensor(res[n][:], res[n][:], pairs(bias), ALU.add).then_inc(res_ready[n], 1)

            def roots(n, g):
                if n in ("pre", "4"):
                    pool.wait_ge(var_ready[n], g + 1)
                    src, power = var[n][:], const[:, C_POW + PAIRS:C_END]
                else:
                    pool.wait_ge(mean_done[n], g + 1)
                    src, power = mv[n][:, :, 1], const[:, C_POW:C_POW + PAIRS]
                if follows(g):
                    pool.wait_ge(z_ready[n], g)
                nc.gpsimd.tensor_tensor(root[n][:], src, power, ALU.pow).then_inc(root_ready[n], 1)

            def layer_output(g):
                pool.wait_ge(xres_loaded, 16 * (g + 1))
                if follows(g):
                    pool.wait_ge(xnew_ready, g)
                nc.gpsimd.tensor_tensor(xb3[:], xres[:], pairs(row("b3")), ALU.add).then_inc(xb3_ready, 1)
                pool.wait_ge(z_ready["3"], g + 1)
                if follows(g):
                    pool.wait_ge(z_ready["4"], g)
                nc.gpsimd.tensor_tensor(xnew[:], z["3"][:], pairs(row("g3")), ALU.mult).then_inc(xz_step, 1)
                pool.wait_ge(xz_step, g + 1)
                pool.wait_ge(xb3_ready, g + 1)
                nc.gpsimd.tensor_tensor(xnew[:], xnew[:], xb3[:], ALU.add).then_inc(xnew_ready, 1)

            def conv_bias(g):
                pool.wait_ge(xnew_ready, g + 1)
                if follows(g):
                    pool.wait_ge(pass_ready, g)
                nc.gpsimd.tensor_tensor(xnc[:], xnew[:], pairs(row("conv_b")), ALU.add).then_inc(xnc_ready, 1)

            def weigh_hidden(g):
                pool.wait_ge(cw_ready, g + 1)
                for p in range(PAIRS):
                    pool.wait_ge(hid_ready[p], g + 1)
                    if follows(g):
                        pool.wait_ge(hidT_done, g)
                    nc.gpsimd.tensor_tensor(
                        hidc[:, p].rearrange("p (e i) -> p e i", e=EXP), hid[:, p].rearrange("p (e i) -> p e i", e=EXP),
                        cwh[:, p].rearrange("p (e i) -> p e i", i=1).broadcast_to([P, EXP, INNER]),
                        ALU.mult).then_inc(hidc_ready[p], 1)

            def add_passes(g):
                pool.wait_ge(pass_ready, g + 1)
                if follows(g):
                    pool.wait_ge(out_ready, g)
                nc.gpsimd.tensor_tensor(rest[:], pass_x[:], pass_r[:], ALU.add).then_inc(rest_ready, 1)

            def iteration(t):
                if live(t):
                    residual_self(t)
                if live(t - 4):
                    weigh_hidden(t - 4)
                if live(t - 3):
                    roots("3", t - 3)
                    layer_output(t - 3)
                if live(t - 4):
                    add_passes(t - 4)
                if live(t + 1):
                    roots("pre", t + 1)
                if live(t - 3):
                    roots("4", t - 3)
                if live(t - 2):
                    roots("C", t - 2)
                if live(t - 1):
                    residual("C", "S", row("g1"), res1_b[:], t - 1)
                if live(t - 3):
                    conv_bias(t - 3)
                if live(t - 2):
                    residual("3", "C", row("g2"), res2_b[:], t - 2)
                if live(t):
                    roots("S", t)
                if isinstance(t, int) and t == -1:
                    late_setup()

            run(pool, iteration)

        @block.vector
        def _(dve):
            def chain(s, g, n, done=0):
                at = [done]

                def link(ins):
                    at[0] += 1
                    assert at[0] <= n
                    ins.then_inc(s, 1)
                    dve.wait_ge(s, g * n + at[0])
                return link

            dve.wait_ge(first_loaded, 32)
            nc.vector.tensor_scalar(bqs[:, 0:1], col("sa_bq"), SCALE, None, ALU.mult)
            nc.vector.tensor_scalar(bqs[:, 1:2], col("ca_bq"), SCALE, None, ALU.mult).then_inc(dve_setup, 1)

            def late_setup():
                for b in range(2):
                    nc.vector.tensor_copy(pick_s[:, b * SEQ:(b + 1) * SEQ], const[0:SEQ, 0:SEQ])
                nc.vector.tensor_copy(pick_c[:], const[0:2, C_PAIR:C_PAIR + P])
                for k in range(TAPS):
                    nc.vector.tensor_scalar(diag[:, k, :], ident, col(f"tap{k}"), None, ALU.mult)
                dve.wait_ge(mask_loaded, 32)
                nc.vector.tensor_scalar(neg_s[:], msk_s[:], 0.0, NEG, ALU.is_equal, ALU.mult)
                nc.vector.tensor_scalar(neg_c[:], msk_c[:], 0.0, NEG, ALU.is_equal, ALU.mult).then_inc(dve_setup, 1)
                dve.wait_ge(rows_loaded, 32)

            def soften(t, c):
                ph, g, r = slot(t, c)
                if not live(g):
                    return
                b, back = parity(c), two_back(ph, g, r)
                sc = S_BANK[b][:].rearrange("p (h k) -> p h k", k=SEQ)
                dve.wait_ge(scores_done[ph], ROWS * g + r + 1)
                nc.vector.tensor_reduce(out=rowmax[:, b, :], in_=sc, op=ALU.max, axis=AX_X).then_inc(max_done[ph], 1)
                dve.wait_ge(max_done[ph], ROWS * g + r + 1)
                if back:
                    dve.wait_ge(probT_done[back[0]], back[1])
                nc.vector.tensor_tensor(
                    prob[:, b, :].rearrange("p (h k) -> p h k", k=SEQ), sc,
                    rowmax[:, b, :].rearrange("p (h k) -> p h k", k=1).broadcast_to([P, 8, SEQ]),
                    ALU.subtract).then_inc(shift_done[ph], 1)

            def moments(n, src, g):
                for p in range(PAIRS):
                    last = nc.vector.bn_stats(stats[n][:, p, :], src[:, p, :])
                unit = 16 if n == "pre" else 1
                last.then_inc(stats_done[n], unit)
                settle(dve)
                dve.wait_ge(stats_done[n], unit * (g + 1))
                for p in range(PAIRS):
                    last = nc.vector.bn_aggr(mv[n][:, p, :], stats[n][:, p, :])
                last.then_inc(mean_done[n], 1)
                if n in ("pre", "4"):
                    dve.wait_ge(mean_done[n], g + 1)
                    nc.vector.tensor_scalar(var[n][:], mv[n][:, :, 1], EPS, None, ALU.add).then_inc(var_ready[n], 1)

            def normalise(n, src, dst, g, used, times=1):
                dve.wait_ge(root_ready[n], g + 1)
                scale = root[n]
                if n not in ("pre", "4"):
                    link = chain(inv_step[n], g, 2)
                    link(nc.vector.tensor_scalar(inv[n][:], root[n][:], EPS, None, ALU.add))
                    link(nc.vector.reciprocal(inv[n][:], inv[n][:]))
                    scale = inv[n]
                for s in used:
                    if follows(g):
                        dve.wait_ge(s, g)
                for p in range(PAIRS):
                    last = nc.vector.tensor_scalar(dst[:, p, :], src[:, p, :], mv[n][:, p, 0:1], scale[:, p:p + 1],
                                                   ALU.subtract, ALU.mult)
                last.then_inc(z_ready[n], 1)

            def post_moments(n, psum, g):
                dve.wait_ge(y_done[n], g + 1)
                dve.wait_ge(res_ready[n], g + 1)
                nc.vector.tensor_tensor(y[n][:].rearrange("p a m -> p (a m)"), psum[:, 0:TOK],
                                        res[n][:].rearrange("p a m -> p (a m)"), ALU.add).then_inc(y_ready[n], 1)
                dve.wait_ge(y_ready[n], g + 1)
                moments(n, y[n], g)

            def heads_out(ph, g):
                o = O_BANK[:, 0:2 * HEADS * VW].rearrange("p (h c) -> p h c", c=VW)
                dve.wait_ge(pv_done[ph], ROWS * (g + 1))
                nc.vector.reciprocal(rsum[ph][:], o[:, :, DK]).then_inc(osum_step[ph], 1)
                dve.wait_ge(osum_step[ph], g + 1)
                if follows(g):
                    dve.wait_ge(oT_done[ph], g)
                nc.vector.tensor_tensor(
                    o_tm[ph][:].rearrange("p a (h d) -> p (a h) d", d=DK), o[:, :, 0:DK],
                    rsum[ph][:].rearrange("p (h d) -> p h d", d=1).broadcast_to([P, 2 * HEADS, DK]),
                    ALU.mult).then_inc(o_ready[ph], 1)

            def spread_keys(ph, g):
                dve.wait_ge(kT_ready[ph], g + 1)
                if follows(g):
                    dve.wait_ge(scores_done[ph], ROWS * g)
                for h in range(HR):
                    last = nc.vector.tensor_scalar(kbd[ph][:, h, :], kT[ph][:], headmask[:, h:h + 1], None, ALU.mult)
                last.then_inc(kbd_ready[ph], 1)

            def route_best(g):
                link = chain(route_step, g, 10)
                dve.wait_ge(er_ready, g + 1)
                if follows(g):
                    dve.wait_ge(pass_ready, g)
                link(nc.vector.tensor_scalar(score[:], e_r[:], 1.0, None, ALU.add))
                link(nc.vector.reciprocal(score[:], score[:]))
                nc.vector.tensor_tensor(biased[:], score[:], pairs(rb[:]), ALU.add).then_inc(biased_done, 1)
                settle(dve)
                dve.wait_ge(biased_done, g + 1)
                for p in range(PAIRS):
                    last = nc.vector.max(top[:, p, :], biased[:, p, :])
                last.then_inc(top_done, 1)
                settle(dve)
                dve.wait_ge(top_done, g + 1)
                for p in range(PAIRS):
                    last = nc.vector.max_index(topi[:, p, :], top[:, p, :], biased[:, p, :])
                last.then_inc(topi_done, 1)

            def route_weights(g):
                link = chain(route_step, g, 10, done=2)
                dve.wait_ge(topi_done, g + 1)
                link(nc.vector.tensor_copy(topf[:], topi[:, :, 0:2]))
                for k, pk in enumerate((pick0, pick1)):
                    last = nc.vector.tensor_tensor(pk[:], pairs(iota8), topf[:, :, k:k + 1].broadcast_to([P, PAIRS, NE]),
                                                   ALU.is_equal)
                link(last)
                link(nc.vector.tensor_tensor(pick0[:], pick0[:], pick1[:], ALU.add))
                link(nc.vector.tensor_tensor(chosen[:], pick0[:], score[:], ALU.mult))
                link(nc.vector.tensor_reduce(out=wsum[:], in_=chosen[:], op=ALU.add, axis=AX_X))
                link(nc.vector.tensor_scalar(wsum[:], wsum[:], 1e-9, None, ALU.add))
                link(nc.vector.reciprocal(wsum[:], wsum[:]))
                if follows(g):
                    dve.wait_ge(hidc_ready[PAIRS - 1], g)
                link(nc.vector.tensor_tensor(
                    cw[:], chosen[:], wsum[:].rearrange("p (a m) -> p a m", m=1).broadcast_to([P, PAIRS, NE]), ALU.mult))
                nc.vector.tensor_scalar(cwh[:], cw[:, :, 0:EXP], 0.5, None, ALU.mult)
                nc.vector.tensor_tensor(c46[:], cw[:, :, EXP], cw[:, :, EXP + 2], ALU.add).then_inc(cw_ready, 1)

            def gates(g, psums):
                for p in (1, 0):
                    dve.wait_ge(th_ready[p], g + 1)
                    nc.vector.scalar_tensor_tensor(out=sig[:, p], in0=th[:, p], scalar=1.0, in1=psums[p][:, 0:TOK],
                                                   op0=ALU.add, op1=ALU.mult).then_inc(gate_step[p], 1)
                for p in (1, 0):
                    dve.wait_ge(gate_step[p], g + 1)
                    if follows(g):
                        dve.wait_ge(hidc_ready[p], g)
                    nc.vector.tensor_tensor(hid[:, p], psums[p][:, TOK:2 * TOK], sig[:, p],
                                            ALU.mult).then_inc(hid_ready[p], 1)

            def passes(g):
                dve.wait_ge(xnc_ready, g + 1)
                dve.wait_ge(cw_ready, g + 1)
                if follows(g):
                    dve.wait_ge(rest_ready, g)
                for p in range(PAIRS):
                    nc.vector.scalar_tensor_tensor(out=pass_x[:, p], in0=z["4"][:, p], scalar=c46[:, p:p + 1],
                                                   in1=xnc[:, p], op0=ALU.mult, op1=ALU.add)
                    last = nc.vector.tensor_scalar(pass_r[:, p], z["4"][:, p], 0.0, cw[:, p, EXP + 3:EXP + 4],
                                                   ALU.max, ALU.mult)
                last.then_inc(pass_ready, 1)

            def finish(g):
                dve.wait_ge(acc_done, g + 1)
                dve.wait_ge(rest_ready, g + 1)
                if follows(g):
                    dve.wait_ge(stored, 16 * g)
                nc.vector.tensor_tensor(y_out[:].rearrange("p a m -> p (a m)"), FFB[:, 0:TOK],
                                        rest[:].rearrange("p a m -> p (a m)"), ALU.add).then_inc(out_ready, 1)

            def iteration(t):
                soften(t, 0)
                if live(t - 4):
                    route_weights(t - 4)
                if live(t - 3):
                    post_moments("3", FFB, t - 3)
                soften(t, 1)
                if live(t - 2):
                    heads_out("C", t - 2)
                if live(t - 3):
                    normalise("3", y["3"], z["3"], t - 3, (xnew_ready,))
                if live(t - 4):
                    passes(t - 4)
                if live(t + 1):
                    dve.wait_ge(x_loaded, 16 * (t + 2))
                    moments("pre", x_tm, t + 1)
                soften(t, 2)
                if live(t - 1):
                    spread_keys("C", t - 1)
                if live(t - 3):
                    dve.wait_ge(xnew_ready, t - 2)
                    moments("4", xnew, t - 3)
                soften(t, 3)
                if live(t + 1):
                    normalise("pre", x_tm, xn, t + 1, (zT_done["pre"], res_ready["S"]))
                if live(t - 3):
                    normalise("4", xnew, z["4"], t - 3, (zT_done["4"], pass_ready))
                if live(t - 2):
                    post_moments("C", POST, t - 2)
                soften(t, 4)
                if live(t - 2):
                    normalise("C", y["C"], z["C"], t - 2, (zT_done["C"], res_ready["3"]))
                if live(t - 4):
                    finish(t - 4)
                soften(t, 5)
                if live(t):
                    heads_out("S", t)
                if live(t - 3):
                    gates(t - 3, (FFB, PROJ))
                soften(t, 6)
                if live(t + 1):
                    spread_keys("S", t + 1)
                soften(t, 7)
                if live(t):
                    post_moments("S", POST, t)
                if live(t - 3):
                    route_best(t - 3)
                if live(t):
                    normalise("S", y["S"], z["S"], t, (zT_done["S"], res_ready["C"]))
                if isinstance(t, int) and t == -1:
                    late_setup()

            run(dve, iteration)

        @block.scalar
        def _(act):
            def load_weights():
                act.dma_start(const[:], const_d).then_inc(first_loaded, 16)
                act.dma_start(w["S"]["q"][:], wq_s).then_inc(proj_loaded["S"], 16)
                act.dma_start(w["S"]["v"][:], wv_s).then_inc(proj_loaded["S"], 16)
                act.dma_start(msk_s[:], mask_self).then_inc(mask_loaded, 16)
                act.dma_start(rows[:].rearrange("p a m -> p (a m)"),
                              rows_d.broadcast_to([P, len(ROWV) * P])).then_inc(rows_loaded, 16)
                nc.scalar.preload_act_table_set("exp_and_others")
                act.dma_start(w1_sb[:], w1).then_inc(ffn_loaded, 16)
                act.dma_start(w2_sb[:], w2.rearrange("(c p) n -> p c n", p=P)).then_inc(ffn_loaded, 16)
                act.dma_start(wr_sb[:], wr).then_inc(mix_loaded, 16)
                act.dma_start(wgu_sb[:, 0], wg.rearrange("e h i -> h e i")).then_inc(mix_loaded, 16)
                act.dma_start(wgu_sb[:, 1], wu.rearrange("e h i -> h e i")).then_inc(mix_loaded, 16)
                act.dma_start(wd_sb[:], wd.rearrange("(c e) i h -> (e i) c h", c=2)).then_inc(mix_loaded, 16)

            load_weights()

            def exponentials(t, c):
                ph, g, r = slot(t, c)
                if not live(g):
                    return
                b, back = parity(c), two_back(ph, g, r)
                act.wait_ge(shift_done[ph], ROWS * g + r + 1)
                nc.scalar.activation(prob[:, b, :], prob[:, b, :], ACT.Exp).then_inc(exp_done[ph], 1)

            def copy_probT(t, c):
                ph, g, r = slot(t, c)
                if not live(g):
                    return
                b, back = parity(c), two_back(ph, g, r)
                act.wait_ge(probT_done[ph], ROWS * g + r + 1)
                if back:
                    act.wait_ge(pv_done[back[0]], back[1])
                nc.scalar.activation(probT[:, b, :], PT_BANK[b][:], ACT.Copy).then_inc(probT_copied[ph], 1)

            def keys_queries(ph, g):
                bias = bqs[:, 0:1] if ph == "S" else bqs[:, 1:2]
                if isinstance(g, int) and g == 0:
                    act.wait_ge(dve_setup, 1)
                    act.wait_ge(pool_setup, 1 if ph == "S" else 2)
                act.wait_ge(qk_done[ph], g + 1)
                if follows(g):
                    act.wait_ge(kbd_ready[ph], g)
                nc.scalar.activation(kT[ph][:], PROJ[:, TOK:2 * TOK], ACT.Identity,
                                     bias=col("sa_bk" if ph == "S" else "ca_bk")).then_inc(kT_ready[ph], 1)
                if follows(g):
                    act.wait_ge(scores_done[ph], ROWS * g)
                for r in range(ROWS):
                    rg = slice(32 * r, 32 * r + 32)
                    last = nc.scalar.activation(qz[ph][rg, r, :], PROJ[rg, 0:TOK], ACT.Identity, bias=bias[rg],
                                                scale=SCALE)
                last.then_inc(q_ready[ph], 1)

            def values(ph, g):
                act.wait_ge(v_done[ph], g + 1)
                if follows(g):
                    act.wait_ge(pv_done[ph], ROWS * g)
                for h in range(2):
                    rng = slice(h * SEQ, (h + 1) * SEQ)
                    last = nc.scalar.activation(
                        vbd[ph][rng, :, :, h, 0:DK].rearrange("p b j d -> p (b j) d"),
                        POST2[rng, :].rearrange("p (b d) -> p b d", d=DK), ACT.Copy)
                last.then_inc(vbd_ready[ph], 1)

            def heads_fm(ph, g):
                act.wait_ge(oT_done[ph], g + 1)
                if follows(g):
                    act.wait_ge(y_done[ph], g)
                nc.scalar.activation(oT[ph][:], POST[:, 0:TOK], ACT.Identity,
                                     bias=col("sa_bv" if ph == "S" else "ca_bv")).then_inc(oT_ready[ph], 1)

            def to_fm(n, dst, g, used, gain=None, bias=None):
                act.wait_ge(zT_done[n], g + 1)
                for s in used:
                    if follows(g):
                        act.wait_ge(s, g)
                if gain is None:
                    nc.scalar.activation(dst[:], POST[:, 0:TOK], ACT.Copy).then_inc(zT_ready[n], 1)
                else:
                    nc.scalar.activation(dst[:], POST[:, 0:TOK], ACT.Identity, bias=col(bias),
                                         scale=col(gain)).then_inc(zT_ready[n], 1)

            def context_fm(g):
                act.wait_ge(encT_done, g + 1)
                if follows(g):
                    act.wait_ge(v_done["C"], g)
                nc.scalar.activation(encT[:], POST[:, 0:TOK], ACT.Copy).then_inc(encT_ready, 1)

            def hidden(half, g):
                act.wait_ge(h_done[half], g + 1)
                if follows(g):
                    act.wait_ge(y_done["3"], g)
                for c in range(2):
                    last = nc.scalar.activation(hT[:, 2 * half + c, :], FFB[:, c * TOK:(c + 1) * TOK], ACT.Relu,
                                                bias=col(f"ff{2 * half + c}"))
                last.then_inc(h_ready[half], 1)

            def mixture_fm(g):
                act.wait_ge(zT_done["4"], g + 1)
                if follows(g):
                    act.wait_ge(acc_done, g)
                nc.scalar.activation(z4T[:, :, TAPS - 1:], POST2.rearrange("p (b s) -> p b s", b=BATCH),
                                     ACT.Copy).then_inc(zT_ready["4"], 1)

            def router_exp(g):
                act.wait_ge(logits_done, g + 1)
                if follows(g):
                    act.wait_ge(cw_ready, g)
                nc.scalar.activation(e_r[:].rearrange("p a m -> p (a m)"), FFB[:, 0:PAIRS * NE], ACT.Exp,
                                     scale=-1.0).then_inc(er_ready, 1)

            def gate_tanh(g, p, psum):
                act.wait_ge(gu_done[p], g + 1)
                if follows(g):
                    act.wait_ge(hid_ready[p], g)
                nc.scalar.activation(th[:, p], psum[:, 0:TOK], ACT.Tanh, scale=0.5).then_inc(th_ready[p], 1)

            def hidden_fm(g):
                act.wait_ge(hidT_done, g + 1)
                if follows(g):
                    act.wait_ge(acc_done, g)
                nc.scalar.activation(hidT[:].rearrange("p a c t -> p (a c t)"), PROJ[:], ACT.Copy).then_inc(hidT_ready, 1)

            def iteration(t):
                copy_probT(t, -1)
                exponentials(t, 0)
                if live(t - 1):
                    to_fm("S", src_fm["C"], t - 1, (qk_done["C"],), "g1", "b1")
                    context_fm(t - 1)
                copy_probT(t, 0)
                exponentials(t, 1)
                if live(t - 2):
                    heads_fm("C", t - 2)
                if live(t - 1):
                    values("C", t - 1)
                    keys_queries("C", t - 1)
                copy_probT(t, 1)
                exponentials(t, 2)
                if live(t - 4):
                    hidden_fm(t - 4)
                copy_probT(t, 2)
                exponentials(t, 3)
                copy_probT(t, 3)
                exponentials(t, 4)
                if live(t + 1):
                    to_fm("pre", src_fm["S"], t + 1, (v_done["S"],))
                if live(t - 3):
                    mixture_fm(t - 3)
                copy_probT(t, 4)
                exponentials(t, 5)
                if live(t - 3):
                    router_exp(t - 3)
                    gate_tanh(t - 3, 1, PROJ)
                    gate_tanh(t - 3, 0, FFB)
                if live(t - 2):
                    to_fm("C", x2T, t - 2, (h_done[1],), "g2", "b2")
                copy_probT(t, 5)
                exponentials(t, 6)
                if live(t - 2):
                    hidden(0, t - 2)
                if live(t):
                    heads_fm("S", t)
                if live(t + 1):
                    values("S", t + 1)
                    keys_queries("S", t + 1)
                copy_probT(t, 6)
                exponentials(t, 7)
                if live(t - 2):
                    hidden(1, t - 2)

            run(act, iteration)

        @block.tensor
        def _(pe):
            mm = nc.tensor.matmul
            pe.wait_ge(first_loaded, 32)

            def scores(t, c):
                ph, g, r = slot(t, c)
                if not live(g):
                    return
                s, back = S_BANK[parity(c)], two_back(ph, g, r)
                if isinstance(g, int) and g == 0:
                    pe.wait_ge(dve_setup, 2)
                if ph == "C":
                    settle(pe)
                if back:
                    pe.wait_ge(shift_done[back[0]], back[1])
                if ph == "S":
                    mm(s[:].rearrange("p (h k) -> p h k", k=SEQ), pick_s[:],
                       neg_s[:].rearrange("p (h k) -> p h k", h=1).broadcast_to([SEQ, 8, SEQ]),
                       start=True, stop=False, skip_group_check=True)
                else:
                    for p in range(PAIRS):
                        mm(s[:, p * TOK:(p + 1) * TOK].rearrange("p (h k) -> p h k", k=SEQ), pick_c[:],
                           neg_c[:, g * PAIRS + p, :].rearrange("p (h k) -> p h k", h=1).broadcast_to([2, HR, SEQ])
                           if isinstance(g, int) else
                           neg_c[:, bass.ds(g * PAIRS + p, 1), :].broadcast_to([2, HR, SEQ]),
                           start=p == 0, stop=False, skip_group_check=True)
                if r == 0:
                    pe.wait_ge(q_ready[ph], g + 1)
                    pe.wait_ge(kbd_ready[ph], g + 1)
                for p in range(PAIRS):
                    for b in range(2):
                        tok = slice(p * P + b * SEQ, p * P + (b + 1) * SEQ)
                        last = mm(s[b * SEQ:(b + 1) * SEQ, p * TOK:(p + 1) * TOK].rearrange("p (h k) -> p h k", k=SEQ),
                                  qz[ph][:, r, tok], kbd[ph][:, :, tok], start=False, stop=True, skip_group_check=True)
                last.then_inc(scores_done[ph], 1)

            def turn_probs(t, c):
                ph, g, r = slot(t, c)
                if not live(g):
                    return
                b, back = parity(c), two_back(ph, g, r)
                pe.wait_ge(exp_done[ph], ROWS * g + r + 1)
                if back:
                    pe.wait_ge(probT_copied[back[0]], back[1])
                for j in range(4):
                    last = nc.tensor.transpose(PT_BANK[b][:, j * P:(j + 1) * P], prob[:, b, j * P:(j + 1) * P], ident)
                last.then_inc(probT_done[ph], 1)

            def heads(t, c):
                ph, g, r = slot(t, c)
                if not live(g):
                    return
                b, back = parity(c), two_back(ph, g, r)
                if r == 0:
                    pe.wait_ge(vbd_ready[ph], g + 1)
                    other = ("C", g - 2) if ph == "S" else ("S", g + 1)
                    if live(other[1]):
                        pe.wait_ge(o_ready[other[0]], other[1] + 1)
                    else:
                        if follows(g):
                            pe.wait_ge(o_ready[ph], g)
                pe.wait_ge(probT_copied[ph], ROWS * g + r + 1)
                for p in range(PAIRS):
                    for jj in range(2):
                        for sq in range(2):
                            j = 2 * r + jj
                            o = (p * HEADS + 2 * j) * VW
                            last = mm(O_BANK[sq * SEQ:(sq + 1) * SEQ, o:o + 2 * VW],
                                      probT[:, b, (2 * p + jj) * P + sq * SEQ:(2 * p + jj) * P + (sq + 1) * SEQ],
                                      vbd[ph][:, 2 * p + sq, j].rearrange("p h c -> p (h c)"),
                                      start=True, stop=True)
                last.then_inc(pv_done[ph], 1)

            def attend(t, c):
                scores(t, c)
                turn_probs(t, c - 1)
                heads(t, c - 2)

            def transpose_pairs(dst, src, s):
                for p in range(PAIRS):
                    last = nc.tensor.transpose(dst[:, p * P:(p + 1) * P], src[:, p], ident)
                last.then_inc(s, 1)

            def project_qk(ph, g, t, use):
                if isinstance(t, int):
                    pe.wait_ge(proj_loaded[ph], 64)
                read = last_read(PROJ_USES, use, t)
                if read:
                    pe.wait_ge(*read)
                pe.wait_ge(zT_ready["pre" if ph == "S" else "S"], g + 1)
                if ph == "C":
                    pe.wait_ge(encT_ready, g + 1)
                mm(PROJ[:, 0:TOK], w[ph]["q"][:], src_fm[ph][:], start=True, stop=True)
                mm(PROJ[:, TOK:2 * TOK], w[ph]["k"][:], kv_fm[ph][:], start=True, stop=True).then_inc(qk_done[ph], 1)

            def project_v(ph, g, t, use):
                if isinstance(t, int):
                    pe.wait_ge(proj_loaded[ph], 64)
                read = last_read(POST_USES, use, t)
                if read:
                    pe.wait_ge(*read)
                pe.wait_ge(zT_ready["pre"] if ph == "S" else encT_ready, g + 1)
                wv = w[ph]["v"][:].rearrange("p (j h d) -> p h j d", h=2, d=DK)
                for b in range(BATCH):
                    for h in range(2):
                        last = mm(POST2[h * SEQ:(h + 1) * SEQ, b * SEQ:(b + 1) * SEQ].rearrange("p (j d) -> p j d", d=DK),
                                  kv_fm[ph][:, b * SEQ:(b + 1) * SEQ], wv[:, h], start=True, stop=True)
                last.then_inc(v_done[ph], 1)

            def heads_to_fm(ph, g, t, use):
                read = last_read(POST_USES, use, t)
                if read:
                    pe.wait_ge(*read)
                pe.wait_ge(o_ready[ph], g + 1)
                transpose_pairs(POST, o_tm[ph], oT_done[ph])

            def output_product(ph, g, t, use):
                read = last_read(POST_USES, use, t)
                if read:
                    pe.wait_ge(*read)
                pe.wait_ge(oT_ready[ph], g + 1)
                for p in range(PAIRS):
                    last = mm(POST[:, p * P:(p + 1) * P], oT[ph][:, p * P:(p + 1) * P], w[ph]["o"][:],
                              start=True, stop=True)
                last.then_inc(y_done[ph], 1)

            def z_to_fm(n, src, dst, uses, g, t, use):
                read = last_read(uses, use, t)
                if read:
                    pe.wait_ge(*read)
                pe.wait_ge(z_ready[n], g + 1)
                transpose_pairs(dst, src, zT_done[n])

            def context_to_fm(g, t, use):
                read = last_read(POST_USES, use, t)
                if read:
                    pe.wait_ge(*read)
                pe.wait_ge(ctx_loaded, 16 * (g + 1))
                transpose_pairs(POST, ctx_tm, encT_done)

            def ffn_in(half, g, t, use):
                if isinstance(t, int):
                    pe.wait_ge(ffn_loaded, 32)
                read = last_read(FFB_USES, use, t)
                if read:
                    pe.wait_ge(*read)
                pe.wait_ge(zT_ready["C"], g + 1)
                for c in range(2):
                    k = 2 * half + c
                    last = mm(FFB[:, c * TOK:(c + 1) * TOK], w1_sb[:, k * P:(k + 1) * P], x2T[:], start=True, stop=True)
                last.then_inc(h_done[half], 1)

            def ffn_out(g, t, use):
                read = last_read(FFB_USES, use, t)
                if read:
                    pe.wait_ge(*read)
                pe.wait_ge(h_ready[1], g + 1)
                for p in range(PAIRS):
                    for k in range(FF):
                        last = mm(FFB[:, p * P:(p + 1) * P], hT[:, k, p * P:(p + 1) * P], w2_sb[:, k, :],
                                  start=k == 0, stop=k == FF - 1)
                last.then_inc(y_done["3"], 1)

            def tokens4(p, b, k):
                return z4T[:, 2 * p + b, k:k + SEQ]

            def logits(g, t, use):
                if isinstance(t, int):
                    pe.wait_ge(mix_loaded, 64)
                read = last_read(FFB_USES, use, t)
                if read:
                    pe.wait_ge(*read)
                pe.wait_ge(zT_ready["4"], g + 1)
                for p in range(PAIRS):
                    for b in range(2):
                        last = mm(FFB[b * SEQ:(b + 1) * SEQ, p * NE:(p + 1) * NE], tokens4(p, b, TAPS - 1), wr_sb[:],
                                  start=True, stop=True)
                last.then_inc(logits_done, 1)

            def gate_up(p, dst, uses, g, t, use):
                read = last_read(uses, use, t)
                if read:
                    pe.wait_ge(*read)
                for b in range(2):
                    last = mm(dst[b * SEQ:(b + 1) * SEQ, :], tokens4(p, b, TAPS - 1),
                              wgu_sb[:].rearrange("p a e i -> p (a e i)"), start=True, stop=True)
                last.then_inc(gu_done[p], 1)

            def hidden_to_fm(g, t, use):
                read = last_read(PROJ_USES, use, t)
                if read:
                    pe.wait_ge(*read)
                for p in range(PAIRS):
                    pe.wait_ge(hidc_ready[p], g + 1)
                    for c in range(2):
                        last = nc.tensor.transpose(PROJ[:, (2 * p + c) * P:(2 * p + c + 1) * P],
                                                   hidc[:, p, c * P:(c + 1) * P], ident)
                last.then_inc(hidT_done, 1)

            def mix(g, t, use):
                read = last_read(FFB_USES, use, t)
                if read:
                    pe.wait_ge(*read)
                pe.wait_ge(hidT_ready, g + 1)
                for p in range(PAIRS):
                    tok = slice(p * P, (p + 1) * P)
                    for b in range(2):
                        for k in range(TAPS):
                            mm(FFB[b * SEQ:(b + 1) * SEQ, tok], tokens4(p, b, k), diag[:, k, :],
                               start=k == 0, stop=False, skip_group_check=True)
                    for c in range(2):
                        last = mm(FFB[:, tok], hidT[:, p, c, :], wd_sb[:, c, :], start=False, stop=c == 1,
                                  skip_group_check=True)
                last.then_inc(acc_done, 1)

            def iteration(t):
                attend(t, 0)
                if live(t - 3):
                    ffn_out(t - 3, t, 0)
                if live(t - 1):
                    z_to_fm("S", z["S"], POST, POST_USES, t - 1, t, 0)
                    context_to_fm(t - 1, t, 1)
                attend(t, 1)
                if live(t - 1):
                    project_v("C", t - 1, t, 2)
                if live(t - 2):
                    heads_to_fm("C", t - 2, t, 2)
                if live(t - 1):
                    project_qk("C", t - 1, t, 0)
                attend(t, 2)
                if live(t - 4):
                    hidden_to_fm(t - 4, t, 1)
                attend(t, 3)
                if live(t - 2):
                    output_product("C", t - 2, t, 4)
                if live(t - 4):
                    mix(t - 4, t, 1)
                attend(t, 4)
                if live(t - 3):
                    z_to_fm("4", z["4"], POST2, POST_USES, t - 3, t, 5)
                if live(t + 1):
                    z_to_fm("pre", xn, POST, POST_USES, t + 1, t, 5)
                attend(t, 5)
                if live(t - 3):
                    logits(t - 3, t, 2)
                    gate_up(1, PROJ, PROJ_USES, t - 3, t, 2)
                    gate_up(0, FFB, FFB_USES, t - 3, t, 3)
                if live(t - 2):
                    z_to_fm("C", z["C"], POST, POST_USES, t - 2, t, 7)
                attend(t, 6)
                if live(t - 2):
                    ffn_in(0, t - 2, t, 4)
                if live(t + 1):
                    project_v("S", t + 1, t, 8)
                if live(t):
                    heads_to_fm("S", t, t, 8)
                if live(t + 1):
                    project_qk("S", t + 1, t, 3)
                attend(t, 7)
                if live(t):
                    output_product("S", t, t, 10)
                if live(t - 2):
                    ffn_in(1, t - 2, t, 5)

            run(pe, iteration)


def constants():
    import numpy as np

    c = np.zeros((P, C_END), np.float32)
    c[:, C_ID:C_ID + P] = np.eye(P)
    for p in range(P):
        c[p, C_HEAD + p % 32 // DK] = 1
    c[:, C_IOTA:C_IOTA + NE] = np.arange(NE)
    for b in range(2):
        c[b, C_PAIR + b * SEQ:C_PAIR + (b + 1) * SEQ] = 1
    c[:, C_POW:C_POW + PAIRS] = 0.5
    c[:, C_POW + PAIRS:C_END] = -0.5
    return c


def kernel(**inputs):
    import numpy as np
    import concourse.bacc as bacc
    from concourse.bass_utils import run_bass_kernel_spmd

    i = {k.replace("L0_xattn_", "").replace("L0_ffn_", ""): np.asarray(v) for k, v in inputs.items()}
    ff = i["ff_b1"].reshape(FF, P)
    taps = i["conv_w"].reshape(TAPS, P)
    per_partition = [i[n] for n in COLS[:10]] + [ff[k] for k in range(FF)] + [taps[k] for k in range(TAPS)]
    per_feature = [i[n] for n in ROWV]
    arrays = {
        "x": i["x"], "ctx": i["ctx_1024"], "mask_self": i["mask_SxS2_ik0"], "mask_cross": i["mask_Bx1x1xS2_if1"],
        "wq_s": i["sa_wq"], "wk_s": i["sa_wk"], "wv_s": i["sa_wv"], "wo_s": i["sa_wo"],
        "wq_c": i["ca_wq"], "wk_c": i["ca_wk"], "wv_c": i["ca_wv"], "wo_c": i["ca_wo"],
        "w1": i["ff_w1"], "w2": i["ff_w2"], "wr": i["Wr"], "wg": i["Wg"], "wu": i["Wu"], "wd": i["Wd"],
        "cols_d": np.stack(per_partition, axis=1), "rows_d": np.concatenate(per_feature)[None, :],
        "rb_d": i["router_bias"][None, :], "const_d": constants(),
    }
    nc = bacc.Bacc("TRN2", target_bir_lowering=False, num_devices=1)
    args = {}
    for name, a in arrays.items():
        arrays[name] = a = np.ascontiguousarray(a)
        args[name] = nc.dram_tensor(name, a.shape, mybir.dt.from_np(a.dtype), kind="ExternalInput").ap()
    args["out"] = nc.dram_tensor("out", i["x"].shape, F32, kind="ExternalOutput").ap()
    program(nc, **args)
    r = run_bass_kernel_spmd(nc, [arrays], core_ids=[0])
    return r.results[0]["out"]
```

```python
from contextlib import ExitStack

import concourse.bass as bass
from concourse import mybir

F32 = mybir.dt.float32
BF16 = mybir.dt.bfloat16
I32 = mybir.dt.int32
U32 = mybir.dt.uint32
ALU = mybir.AluOpType
ACT = mybir.ActivationFunctionType
AX_X = mybir.AxisListType.X

P = 128
SEQ = 64
HEADS, DK = 16, 8
PAIRS = 2
TOK = PAIRS * P
BATCH = TOK // SEQ
ROWS = 4
HR = HEADS // ROWS
FF = 4
EXP, INNER = 4, 64
NE = 8
TAPS = 4
VW = DK + 1
NEG = -float(2 ** 100)
EPS = 1e-5

COLS = ["sa_bq", "sa_bk", "sa_bv", "ca_bq", "ca_bk", "ca_bv", "g1", "b1", "g2", "b2",
        "ff0", "ff1", "ff2", "ff3", "tap0", "tap1", "tap2", "tap3"]
ROWV = ["sa_bo", "g1", "b1", "ca_bo", "g2", "b2", "ff_b2", "g3", "b3", "conv_b"]
C_ID, C_HEAD, C_IOTA, C_PAIR, C_POW = 0, P, P + HR, P + HR + NE, P + HR + NE + P
C_END = C_POW + 2 * PAIRS


def program(nc, x, ctx, mask_self, mask_cross, wq_s, wk_s, wv_s, wo_s, wq_c, wk_c, wv_c, wo_c,
            w1, w2, wr, wg, wu, wd, cols_d, rows_d, rb_d, const_d, out):
    GROUPS = x.shape[0] * SEQ // TOK
    SCALE = float(DK) ** -0.5

    def by_group(a):
        return a.rearrange("b s d -> (b s) d").rearrange("(g p t) d -> g t p d", p=PAIRS, t=P)

    x_g, ctx_g, out_g = by_group(x), by_group(ctx), by_group(out)

    with ExitStack() as stack:
        def sb(name, shape, dt=F32):
            return stack.enter_context(nc.sbuf_tensor(name, shape, dt))

        def sem(name):
            return stack.enter_context(nc.semaphore(name))

        bank = [stack.enter_context(nc.psum_tensor(f"bank{i}", [P, 512], F32)) for i in range(8)]
        S_BANK, PT_BANK = bank[0:2], bank[2:4]
        O_BANK, PROJ, POST, FFB = bank[4:8]
        POST2 = POST[:, TOK:2 * TOK]

        w = {"S": {}, "C": {}}
        for ph in "SC":
            for n in ("q", "k", "v", "o"):
                w[ph][n] = sb(f"w{n}_{ph}", [P, P])
        w1_sb = sb("w1_sb", [P, FF * P])
        w2_sb = sb("w2_sb", [P, FF, P])
        wr_sb = sb("wr_sb", [P, NE])
        wgu_sb = sb("wgu_sb", [P, 2, EXP, INNER])
        wd_sb = sb("wd_sb", [P, 2, P])
        cols = sb("cols", [P, len(COLS)])
        rows = sb("rows", [P, len(ROWV), P])
        rb = sb("rb", [P, NE])
        const = sb("const", [P, C_END])
        msk_s = sb("msk_s", [SEQ, SEQ], I32)
        msk_c = sb("msk_c", [2, GROUPS * PAIRS, SEQ], I32)
        neg_s = sb("neg_s", [SEQ, SEQ], BF16)
        neg_c = sb("neg_c", [2, GROUPS * PAIRS, SEQ], BF16)
        pick_s = sb("pick_s", [SEQ, P], BF16)
        pick_c = sb("pick_c", [2, P], BF16)
        bqs = sb("bqs", [P, 2])
        res1_b = sb("res1_b", [P, P])
        res2_b = sb("res2_b", [P, P])
        ident = const[:, C_ID:C_ID + P]
        headmask = const[:, C_HEAD:C_HEAD + HR]
        iota8 = const[:, C_IOTA:C_IOTA + NE]

        def col(name):
            return cols[:, COLS.index(name):COLS.index(name) + 1]

        def row(name):
            return rows[:, ROWV.index(name), :]

        def pairs(r, n=PAIRS):
            return r.rearrange("p (a m) -> p a m", a=1).broadcast_to([P, n, r.shape[1]])

        x_tm = sb("x_tm", [P, PAIRS, P])
        ctx_tm = sb("ctx_tm", [P, PAIRS, P])
        xres = sb("xres", [P, PAIRS, P])
        xn = sb("xn", [P, PAIRS, P])
        src_fm = {"S": sb("xnT", [P, TOK]), "C": sb("x1T", [P, TOK])}
        encT = sb("encT", [P, TOK])
        kv_fm = {"S": src_fm["S"], "C": encT}
        x2T = sb("x2T", [P, TOK])
        qz = {ph: sb(f"qz_{ph}", [P, ROWS, TOK]) for ph in "SC"}
        kT = {ph: sb(f"kT_{ph}", [P, TOK]) for ph in "SC"}
        kbd = {ph: sb(f"kbd_{ph}", [P, HR, TOK]) for ph in "SC"}
        vbd = {ph: sb(f"vbd_{ph}", [P, BATCH, HEADS // 2, 2, VW]) for ph in "SC"}
        rowmax = sb("rowmax", [P, 2, 8])
        prob = sb("prob", [P, 2, 512])
        probT = sb("probT", [P, 2, 512])
        rsum = {ph: sb(f"rsum_{ph}", [P, 2 * HEADS]) for ph in "SC"}
        o_tm = {ph: sb(f"o_tm_{ph}", [P, PAIRS, P]) for ph in "SC"}
        oT = {ph: sb(f"oT_{ph}", [P, TOK]) for ph in "SC"}
        LN = ("pre", "S", "C", "3", "4")
        y = {n: sb(f"y_{n}", [P, PAIRS, P]) for n in ("S", "C", "3")}
        z = {n: sb(f"z_{n}", [P, PAIRS, P]) for n in ("S", "C", "3", "4")}
        res = {n: sb(f"res_{n}", [P, PAIRS, P]) for n in ("S", "C", "3")}
        stats = {n: sb(f"stats_{n}", [P, PAIRS, 6]) for n in LN}
        mv = {n: sb(f"mv_{n}", [P, PAIRS, 2]) for n in LN}
        var = {n: sb(f"var_{n}", [P, PAIRS]) for n in LN}
        root = {n: sb(f"root_{n}", [P, PAIRS]) for n in LN}
        inv = {n: sb(f"inv_{n}", [P, PAIRS]) for n in LN}
        hT = sb("hT", [P, FF, TOK])
        xb3 = sb("xb3", [P, PAIRS, P])
        xnew = sb("xnew", [P, PAIRS, P])
        xnc = sb("xnc", [P, PAIRS, P])
        z4T = sb("z4T", [P, BATCH, TAPS - 1 + SEQ])
        tapped = sb("tapped", [P, TAPS, TOK])
        conv2 = sb("conv2", [P, 2, TOK])
        convT = sb("convT", [P, TOK])
        e_r = sb("e_r", [P, PAIRS, NE])
        score = sb("score", [P, PAIRS, NE])
        biased = sb("biased", [P, PAIRS, NE])
        top = sb("top", [P, PAIRS, 8])
        topi = sb("topi", [P, PAIRS, 8], U32)
        pick0 = sb("pick0", [P, PAIRS, NE])
        pick1 = sb("pick1", [P, PAIRS, NE])
        chosen = sb("chosen", [P, PAIRS, NE])
        wsum = sb("wsum", [P, PAIRS])
        cw = sb("cw", [P, PAIRS, NE])
        cwh = sb("cwh", [P, PAIRS, EXP])
        c46 = sb("c46", [P, PAIRS])
        th = sb("th", [P, PAIRS, EXP * INNER])
        sig = sb("sig", [P, PAIRS, EXP * INNER])
        hid = sb("hid", [P, PAIRS, EXP * INNER])
        hidc = sb("hidc", [P, PAIRS, EXP * INNER])
        hidT = sb("hidT", [P, PAIRS, 2, P])
        pass_x = sb("pass_x", [P, PAIRS, P])
        pass_r = sb("pass_r", [P, PAIRS, P])
        rest = sb("rest", [P, PAIRS, P])
        y_out = sb("y_out", [P, PAIRS, P])

        first_loaded, mask_loaded, rows_loaded = sem("first_loaded"), sem("mask_loaded"), sem("rows_loaded")
        ffn_loaded, mix_loaded = sem("ffn_loaded"), sem("mix_loaded")
        x_loaded, ctx_loaded, xres_loaded, stored = (sem(n) for n in
                                                     ("x_loaded", "ctx_loaded", "xres_loaded", "stored"))
        dve_setup, pool_setup, setup_step = sem("dve_setup"), sem("pool_setup"), sem("setup_step")

        def both(name):
            return {ph: sem(f"{name}_{ph}") for ph in "SC"}

        proj_loaded = both("proj_loaded")
        scores_done, max_done, shift_done, exp_done = (both(n) for n in ("scores", "max", "shift", "exp"))
        probT_done, probT_copied, pv_done = (both(n) for n in ("probT", "probTc", "pv"))
        qk_done, v_done, q_ready = (both(n) for n in ("qk", "v", "q"))
        kT_ready, kbd_ready, vbd_ready = (both(n) for n in ("kT", "kbd", "vbd"))
        osum_step, o_ready, oT_done, oT_ready = (both(n) for n in ("osum", "o", "oTps", "oT"))
        y_done = {n: sem(f"yps_{n}") for n in ("S", "C", "3")}
        y_ready = {n: sem(f"y_{n}r") for n in ("S", "C", "3")}
        res_step = {n: sem(f"res_step_{n}") for n in ("S", "C", "3")}
        res_ready = {n: sem(f"res_{n}r") for n in ("S", "C", "3")}
        stats_done = {n: sem(f"stats_{n}d") for n in LN}
        mean_done = {n: sem(f"mean_{n}d") for n in LN}
        var_ready = {n: sem(f"var_{n}r") for n in LN}
        root_ready = {n: sem(f"root_{n}r") for n in LN}
        inv_step = {n: sem(f"inv_step_{n}") for n in LN}
        z_ready = {n: sem(f"z_{n}r") for n in LN}
        zT_done = {n: sem(f"zTps_{n}") for n in LN}
        zT_ready = {n: sem(f"zT_{n}r") for n in LN}
        encT_done, encT_ready = sem("encTps"), sem("encT_ready")
        h_done = [sem("h_ps0"), sem("h_ps1")]
        h_ready = [sem("h_ready0"), sem("h_ready1")]
        xb3_ready, xz_step, xnew_ready, xnc_ready = (sem(n) for n in ("xb3", "xz_step", "xnew_r", "xnc_r"))
        logits_done, er_ready, route_step, cw_ready = (sem(n) for n in ("logits", "er", "route_step", "cw"))
        biased_done, top_done, topi_done = sem("biased_d"), sem("top_d"), sem("topi_d")
        gu_done = [sem("gu_ps0"), sem("gu_ps1")]
        th_ready = [sem("th0"), sem("th1")]
        gate_step = [sem("gate_step0"), sem("gate_step1")]
        hid_ready = [sem("hid0"), sem("hid1")]
        hidc_ready = [sem("hidc0"), sem("hidc1")]
        tapped_ready, conv_step, conv_ready = sem("tapped"), sem("conv_step"), sem("conv_ready")
        hidT_done, hidT_ready, acc_done = sem("hidTps"), sem("hidT_ready"), sem("acc")
        pass_ready, rest_step, rest_ready, out_ready = (sem(n) for n in ("pass_ready", "rest_step", "rest", "out_sem"))

        def live(g):
            return not isinstance(g, int) or 0 <= g < GROUPS

        def follows(g):
            return not isinstance(g, int) or g >= 1

        def slot(t, c):
            if c < 0:
                t, c = t - 1, c + 2 * ROWS
            return ("S", t, c) if c < ROWS else ("C", t - 1, c - ROWS)

        def two_back(ph, g, r):
            if r >= 2:
                return ph, ROWS * g + r - 1
            other, og = ("C", g - 2) if ph == "S" else ("S", g + 1)
            if not live(og):
                other, og = ph, g - 1
            return (other, ROWS * og + r + 3) if live(og) else None

        def parity(r):
            return r % 2

        PROJ_USES = ([(q_ready["C"], -1), (hidT_ready, -4), (hid_ready[1], -3), (q_ready["S"], 1)],
                     [(hidT_ready, -4), (h_ready[1], -2)])
        POST_USES = ([(zT_ready["S"], -1), (encT_ready, -1), (oT_ready["C"], -2), (vbd_ready["C"], -1),
                      (y_ready["C"], -2), (zT_ready["pre"], 1), (zT_ready["4"], -3), (zT_ready["C"], -2),
                      (er_ready, -3), (oT_ready["S"], 0), (vbd_ready["S"], 1), (y_ready["S"], 0)],
                     [(oT_ready["C"], -2), (y_ready["C"], -2), (zT_ready["C"], -2)])
        FFB_USES = ([(y_ready["3"], -3), (out_ready, -4), (hid_ready[0], -3), (h_ready[0], -2), (h_ready[1], -2)],
                    [(y_ready["3"], -3), (h_ready[0], -2)])
        GATE_USES = [([], [(hid_ready[p], -3)]) for p in range(PAIRS)]
        LOGIT_USES = ([], [(er_ready, -3)])
        TOKEN_USES = ([], [(zT_ready["4"], -3)])
        SUM_USES = ([], [(out_ready, -4)])

        def last_read(uses, n, t):
            for back in range(3):
                order = uses[1 if isinstance(t, int) and t - back > GROUPS else 0]
                for s, off in reversed(order[:n] if back == 0 else order):
                    if live(t - back + off):
                        return s, t - back + off + 1
            return None

        def settle(eng):
            eng.wait_ge(first_loaded, 32)

        block = stack.enter_context(nc.Block())

        def run(eng, iteration, drain):
            first, last = 4, GROUPS - 2
            for t in range(-1, first):
                iteration(t)
            with eng.Fori(first, last) as t:
                iteration(t)
            for t in range(last, GROUPS + 1):
                iteration(t)
            for t in range(GROUPS + 1, GROUPS + 4):
                drain(t)

        @block.sync
        def _(sp):
            def load_x(g):
                if follows(g):
                    sp.wait_ge(z_ready["pre"], g)
                sp.dma_start(x_tm[:], x_g[g]).then_inc(x_loaded, 16)

            def load_ctx(g):
                if follows(g):
                    sp.wait_ge(encT_done, g)
                sp.dma_start(ctx_tm[:], ctx_g[g]).then_inc(ctx_loaded, 16)

            def load_xres(g):
                if follows(g):
                    sp.wait_ge(xb3_ready, g)
                sp.dma_start(xres[:], x_g[g]).then_inc(xres_loaded, 16)

            load_x(0)
            sp.dma_start(cols[:], cols_d).then_inc(first_loaded, 16)
            sp.dma_start(w["S"]["k"][:], wk_s).then_inc(proj_loaded["S"], 16)
            sp.dma_start(msk_c[:], mask_cross.rearrange("(t b) i j k -> b t (i j k)", b=2)).then_inc(mask_loaded, 16)
            load_x(1)
            sp.dma_start(rows[:].rearrange("p a m -> p (a m)"),
                         rows_d.broadcast_to([P, len(ROWV) * P])).then_inc(rows_loaded, 16)
            sp.dma_start(rb[:], rb_d.broadcast_to([P, NE])).then_inc(rows_loaded, 16)
            for dst, a in ((w["S"]["o"], wo_s), (w["C"]["q"], wq_c), (w["C"]["k"], wk_c), (w["C"]["v"], wv_c),
                           (w["C"]["o"], wo_c)):
                sp.dma_start(dst[:], a).then_inc(proj_loaded["C"], 16)
            sp.dma_start(w1_sb[:], w1).then_inc(ffn_loaded, 16)
            sp.dma_start(w2_sb[:], w2.rearrange("(c p) n -> p c n", p=P)).then_inc(ffn_loaded, 16)
            sp.dma_start(wr_sb[:], wr).then_inc(mix_loaded, 16)
            sp.dma_start(wgu_sb[:, 0], wg.rearrange("e h i -> h e i")).then_inc(mix_loaded, 16)
            sp.dma_start(wgu_sb[:, 1], wu.rearrange("e h i -> h e i")).then_inc(mix_loaded, 16)
            sp.dma_start(wd_sb[:], wd.rearrange("(c e) i h -> (e i) c h", c=2)).then_inc(mix_loaded, 16)

            def iteration(t):
                if live(t):
                    load_ctx(t)
                if live(t - 2):
                    load_xres(t - 2)
                if live(t - 4):
                    sp.wait_ge(out_ready, t - 3)
                    sp.dma_start(out_g[t - 4], y_out[:]).then_inc(stored, 16)
                if live(t + 2) and not (isinstance(t, int) and t < 0):
                    load_x(t + 2)

            run(sp, iteration, iteration)
            sp.wait_ge(stored, 16 * GROUPS)

        @block.gpsimd
        def _(pool):
            def clear(ph, zeros, step):
                for buf in zeros:
                    last = nc.gpsimd.memset(buf[:], 0.0)
                last.then_inc(setup_step, 1)
                pool.wait_ge(setup_step, step)
                nc.gpsimd.memset(vbd[ph][0:SEQ, :, :, 0, DK:VW], 1.0)
                nc.gpsimd.memset(vbd[ph][SEQ:P, :, :, 1, DK:VW], 1.0).then_inc(pool_setup, 1)

            def late_setup():
                clear("C", (qz["C"], vbd["C"], z4T), 2)
                pool.wait_ge(pool_setup, 2)
                pool.wait_ge(rows_loaded, 32)
                nc.gpsimd.tensor_tensor(res1_b[:], row("b1"), row("ca_bo"), ALU.add)
                nc.gpsimd.tensor_tensor(res2_b[:], row("b2"), row("ff_b2"), ALU.add).then_inc(setup_step, 1)
                pool.wait_ge(setup_step, 3)

            clear("S", (qz["S"], vbd["S"]), 1)
            pool.wait_ge(pool_setup, 1)
            pool.wait_ge(first_loaded, 32)

            def residual_self(g):
                pool.wait_ge(z_ready["pre"], g + 1)
                if follows(g):
                    pool.wait_ge(y_ready["S"], g)
                nc.gpsimd.tensor_tensor(res["S"][:], xn[:], pairs(row("sa_bo")), ALU.add).then_inc(res_ready["S"], 1)

            def residual(n, frm, gain, bias, g):
                pool.wait_ge(z_ready[frm], g + 1)
                if follows(g):
                    pool.wait_ge(y_ready[n], g)
                nc.gpsimd.tensor_tensor(res[n][:], z[frm][:], pairs(gain), ALU.mult).then_inc(res_step[n], 1)
                pool.wait_ge(res_step[n], g + 1)
                nc.gpsimd.tensor_tensor(res[n][:], res[n][:], pairs(bias), ALU.add).then_inc(res_ready[n], 1)

            def roots(n, g):
                if n in ("pre", "4"):
                    pool.wait_ge(var_ready[n], g + 1)
                    src, power = var[n][:], const[:, C_POW + PAIRS:C_END]
                else:
                    pool.wait_ge(mean_done[n], g + 1)
                    src, power = mv[n][:, :, 1], const[:, C_POW:C_POW + PAIRS]
                if follows(g):
                    pool.wait_ge(z_ready[n], g)
                nc.gpsimd.tensor_tensor(root[n][:], src, power, ALU.pow).then_inc(root_ready[n], 1)

            def layer_output(g):
                pool.wait_ge(xres_loaded, 16 * (g + 1))
                if follows(g):
                    pool.wait_ge(xnew_ready, g)
                nc.gpsimd.tensor_tensor(xb3[:], xres[:], pairs(row("b3")), ALU.add).then_inc(xb3_ready, 1)
                pool.wait_ge(z_ready["3"], g + 1)
                if follows(g):
                    pool.wait_ge(z_ready["4"], g)
                nc.gpsimd.tensor_tensor(xnew[:], z["3"][:], pairs(row("g3")), ALU.mult).then_inc(xz_step, 1)
                pool.wait_ge(xz_step, g + 1)
                pool.wait_ge(xb3_ready, g + 1)
                nc.gpsimd.tensor_tensor(xnew[:], xnew[:], xb3[:], ALU.add).then_inc(xnew_ready, 1)

            def conv_bias(g):
                pool.wait_ge(xnew_ready, g + 1)
                if follows(g):
                    pool.wait_ge(rest_ready, g)
                nc.gpsimd.tensor_tensor(xnc[:], xnew[:], pairs(row("conv_b")), ALU.add).then_inc(xnc_ready, 1)

            def add_taps(g):
                pool.wait_ge(tapped_ready, g + 1)
                if follows(g):
                    pool.wait_ge(conv_ready, g)
                nc.gpsimd.tensor_tensor(conv2[:], tapped[:, 0:2, :], tapped[:, 2:4, :], ALU.add).then_inc(conv_step, 1)
                pool.wait_ge(conv_step, g + 1)
                if follows(g):
                    pool.wait_ge(acc_done, g)
                nc.gpsimd.tensor_tensor(convT[:], conv2[:, 0, :], conv2[:, 1, :], ALU.add).then_inc(conv_ready, 1)

            def weigh_hidden(g):
                pool.wait_ge(cw_ready, g + 1)
                for p in range(PAIRS):
                    pool.wait_ge(hid_ready[p], g + 1)
                    if follows(g):
                        pool.wait_ge(hidT_done, g)
                    nc.gpsimd.tensor_tensor(
                        hidc[:, p].rearrange("p (e i) -> p e i", e=EXP), hid[:, p].rearrange("p (e i) -> p e i", e=EXP),
                        cwh[:, p].rearrange("p (e i) -> p e i", i=1).broadcast_to([P, EXP, INNER]),
                        ALU.mult).then_inc(hidc_ready[p], 1)

            def add_passes(g):
                pool.wait_ge(pass_ready, g + 1)
                if follows(g):
                    pool.wait_ge(out_ready, g)
                nc.gpsimd.tensor_tensor(rest[:], pass_x[:], pass_r[:], ALU.add).then_inc(rest_step, 1)
                pool.wait_ge(rest_step, g + 1)
                pool.wait_ge(xnc_ready, g + 1)
                nc.gpsimd.tensor_tensor(rest[:], rest[:], xnc[:], ALU.add).then_inc(rest_ready, 1)

            def iteration(t):
                if live(t - 4):
                    weigh_hidden(t - 4)
                if live(t - 3):
                    roots("3", t - 3)
                    layer_output(t - 3)
                if live(t):
                    residual_self(t)
                if live(t + 1):
                    roots("pre", t + 1)
                if live(t - 3):
                    roots("4", t - 3)
                if live(t - 4):
                    add_passes(t - 4)
                if live(t - 2):
                    roots("C", t - 2)
                if live(t - 1):
                    residual("C", "S", row("g1"), res1_b[:], t - 1)
                if live(t - 3):
                    conv_bias(t - 3)
                if isinstance(t, int) and t == -1:
                    late_setup()
                if live(t):
                    roots("S", t)
                if live(t - 2):
                    residual("3", "C", row("g2"), res2_b[:], t - 2)
                if live(t - 3):
                    add_taps(t - 3)

            def drain(t):
                if live(t - 4):
                    weigh_hidden(t - 4)
                if live(t - 3):
                    roots("3", t - 3)
                    layer_output(t - 3)
                if live(t - 2):
                    roots("C", t - 2)
                if live(t - 3):
                    roots("4", t - 3)
                if live(t - 4):
                    add_passes(t - 4)
                if live(t - 3):
                    add_taps(t - 3)
                    conv_bias(t - 3)
                if live(t - 2):
                    residual("3", "C", row("g2"), res2_b[:], t - 2)

            run(pool, iteration, drain)

        @block.vector
        def _(dve):
            def chain(s, g, n, done=0):
                at = [done]

                def link(ins):
                    at[0] += 1
                    assert at[0] <= n
                    ins.then_inc(s, 1)
                    dve.wait_ge(s, g * n + at[0])
                return link

            dve.wait_ge(first_loaded, 32)
            nc.vector.tensor_scalar(bqs[:, 0:1], col("sa_bq"), SCALE, None, ALU.mult)
            nc.vector.tensor_scalar(bqs[:, 1:2], col("ca_bq"), SCALE, None, ALU.mult).then_inc(dve_setup, 1)

            def late_setup():
                for b in range(2):
                    nc.vector.tensor_copy(pick_s[:, b * SEQ:(b + 1) * SEQ], const[0:SEQ, 0:SEQ])
                nc.vector.tensor_copy(pick_c[:], const[0:2, C_PAIR:C_PAIR + P])
                dve.wait_ge(mask_loaded, 32)
                nc.vector.tensor_scalar(neg_s[:], msk_s[:], 0.0, NEG, ALU.is_equal, ALU.mult)
                nc.vector.tensor_scalar(neg_c[:], msk_c[:], 0.0, NEG, ALU.is_equal, ALU.mult).then_inc(dve_setup, 1)
                dve.wait_ge(rows_loaded, 32)

            def soften(t, c):
                ph, g, r = slot(t, c)
                if not live(g):
                    return
                b, back = parity(c), two_back(ph, g, r)
                sc = S_BANK[b][:].rearrange("p (h k) -> p h k", k=SEQ)
                dve.wait_ge(scores_done[ph], ROWS * g + r + 1)
                nc.vector.tensor_reduce(out=rowmax[:, b, :], in_=sc, op=ALU.max, axis=AX_X).then_inc(max_done[ph], 1)
                dve.wait_ge(max_done[ph], ROWS * g + r + 1)
                if back:
                    dve.wait_ge(probT_done[back[0]], back[1])
                nc.vector.tensor_tensor(
                    prob[:, b, :].rearrange("p (h k) -> p h k", k=SEQ), sc,
                    rowmax[:, b, :].rearrange("p (h k) -> p h k", k=1).broadcast_to([P, 8, SEQ]),
                    ALU.subtract).then_inc(shift_done[ph], 1)

            def moments(n, src, g):
                for p in range(PAIRS):
                    last = nc.vector.bn_stats(stats[n][:, p, :], src[:, p, :])
                unit = 16 if n == "pre" else 1
                last.then_inc(stats_done[n], unit)
                settle(dve)
                dve.wait_ge(stats_done[n], unit * (g + 1))
                for p in range(PAIRS):
                    last = nc.vector.bn_aggr(mv[n][:, p, :], stats[n][:, p, :])
                last.then_inc(mean_done[n], 1)
                if n in ("pre", "4"):
                    dve.wait_ge(mean_done[n], g + 1)
                    nc.vector.tensor_scalar(var[n][:], mv[n][:, :, 1], EPS, None, ALU.add).then_inc(var_ready[n], 1)

            def normalise(n, src, dst, g, used, times=1):
                dve.wait_ge(root_ready[n], g + 1)
                scale = root[n]
                if n not in ("pre", "4"):
                    link = chain(inv_step[n], g, 2)
                    link(nc.vector.tensor_scalar(inv[n][:], root[n][:], EPS, None, ALU.add))
                    link(nc.vector.reciprocal(inv[n][:], inv[n][:]))
                    scale = inv[n]
                for s in used:
                    if follows(g):
                        dve.wait_ge(s, g)
                for p in range(PAIRS):
                    last = nc.vector.tensor_scalar(dst[:, p, :], src[:, p, :], mv[n][:, p, 0:1], scale[:, p:p + 1],
                                                   ALU.subtract, ALU.mult)
                last.then_inc(z_ready[n], 1)

            def post_moments(n, psum, g):
                dve.wait_ge(y_done[n], g + 1)
                dve.wait_ge(res_ready[n], g + 1)
                nc.vector.tensor_tensor(y[n][:].rearrange("p a m -> p (a m)"), psum[:, 0:TOK],
                                        res[n][:].rearrange("p a m -> p (a m)"), ALU.add).then_inc(y_ready[n], 1)
                dve.wait_ge(y_ready[n], g + 1)
                moments(n, y[n], g)

            def heads_out(ph, g):
                o = O_BANK[:, 0:2 * HEADS * VW].rearrange("p (h c) -> p h c", c=VW)
                dve.wait_ge(pv_done[ph], ROWS * (g + 1))
                nc.vector.reciprocal(rsum[ph][:], o[:, :, DK]).then_inc(osum_step[ph], 1)
                dve.wait_ge(osum_step[ph], g + 1)
                if follows(g):
                    dve.wait_ge(oT_done[ph], g)
                nc.vector.tensor_tensor(
                    o_tm[ph][:].rearrange("p a (h d) -> p (a h) d", d=DK), o[:, :, 0:DK],
                    rsum[ph][:].rearrange("p (h d) -> p h d", d=1).broadcast_to([P, 2 * HEADS, DK]),
                    ALU.mult).then_inc(o_ready[ph], 1)

            def spread_keys(ph, g):
                dve.wait_ge(kT_ready[ph], g + 1)
                if follows(g):
                    dve.wait_ge(scores_done[ph], ROWS * g)
                for h in range(HR):
                    last = nc.vector.tensor_scalar(kbd[ph][:, h, :], kT[ph][:], headmask[:, h:h + 1], None, ALU.mult)
                last.then_inc(kbd_ready[ph], 1)

            def route_best(g):
                link = chain(route_step, g, 9)
                dve.wait_ge(er_ready, g + 1)
                link(nc.vector.tensor_scalar(score[:], e_r[:], 1.0, None, ALU.add))
                link(nc.vector.reciprocal(score[:], score[:]))
                nc.vector.tensor_tensor(biased[:], score[:], pairs(rb[:]), ALU.add).then_inc(biased_done, 1)
                settle(dve)
                dve.wait_ge(biased_done, g + 1)
                for p in range(PAIRS):
                    last = nc.vector.max(top[:, p, :], biased[:, p, :])
                last.then_inc(top_done, 1)
                settle(dve)
                dve.wait_ge(top_done, g + 1)
                for p in range(PAIRS):
                    last = nc.vector.max_index(topi[:, p, :], top[:, p, :], biased[:, p, :])
                last.then_inc(topi_done, 1)

            def route_weights(g):
                link = chain(route_step, g, 9, done=2)
                dve.wait_ge(topi_done, g + 1)
                for k, pk in enumerate((pick0, pick1)):
                    last = nc.vector.tensor_tensor(pk[:], pairs(iota8), topi[:, :, k:k + 1].broadcast_to([P, PAIRS, NE]),
                                                   ALU.is_equal)
                link(last)
                link(nc.vector.tensor_tensor(pick0[:], pick0[:], pick1[:], ALU.add))
                link(nc.vector.tensor_tensor(chosen[:], pick0[:], score[:], ALU.mult))
                link(nc.vector.tensor_reduce(out=wsum[:], in_=chosen[:], op=ALU.add, axis=AX_X))
                link(nc.vector.tensor_scalar(wsum[:], wsum[:], 1e-9, None, ALU.add))
                link(nc.vector.reciprocal(wsum[:], wsum[:]))
                if follows(g):
                    dve.wait_ge(hidc_ready[PAIRS - 1], g)
                    dve.wait_ge(pass_ready, g)
                link(nc.vector.tensor_tensor(
                    cw[:], chosen[:], wsum[:].rearrange("p (a m) -> p a m", m=1).broadcast_to([P, PAIRS, NE]), ALU.mult))
                nc.vector.tensor_scalar(cwh[:], cw[:, :, 0:EXP], 0.5, None, ALU.mult)
                nc.vector.tensor_tensor(c46[:], cw[:, :, EXP], cw[:, :, EXP + 2], ALU.add).then_inc(cw_ready, 1)

            def gates(g, psums):
                for p in (1, 0):
                    dve.wait_ge(th_ready[p], g + 1)
                    nc.vector.scalar_tensor_tensor(out=sig[:, p], in0=th[:, p], scalar=1.0, in1=psums[p][:, 0:TOK],
                                                   op0=ALU.add, op1=ALU.mult).then_inc(gate_step[p], 1)
                for p in (1, 0):
                    dve.wait_ge(gate_step[p], g + 1)
                    if follows(g):
                        dve.wait_ge(hidc_ready[p], g)
                    nc.vector.tensor_tensor(hid[:, p], psums[p][:, TOK:2 * TOK], sig[:, p],
                                            ALU.mult).then_inc(hid_ready[p], 1)

            def finish(g, psum):
                dve.wait_ge(acc_done, g + 1)
                dve.wait_ge(rest_ready, g + 1)
                if follows(g):
                    dve.wait_ge(stored, 16 * g)
                nc.vector.tensor_tensor(y_out[:].rearrange("p a m -> p (a m)"), psum[:, 0:TOK],
                                        rest[:].rearrange("p a m -> p (a m)"), ALU.add).then_inc(out_ready, 1)

            def iteration(t):
                soften(t, 0)
                if live(t - 4):
                    route_weights(t - 4)
                if live(t - 3):
                    post_moments("3", FFB, t - 3)
                soften(t, 1)
                if live(t - 2):
                    heads_out("C", t - 2)
                if live(t + 1):
                    dve.wait_ge(x_loaded, 16 * (t + 2))
                    moments("pre", x_tm, t + 1)
                if live(t - 3):
                    normalise("3", y["3"], z["3"], t - 3, (xnew_ready,))
                soften(t, 2)
                if live(t - 1):
                    spread_keys("C", t - 1)
                if live(t - 3):
                    dve.wait_ge(xnew_ready, t - 2)
                    moments("4", xnew, t - 3)
                soften(t, 3)
                if live(t + 1):
                    normalise("pre", x_tm, xn, t + 1, (zT_done["pre"], res_ready["S"]))
                if live(t - 3):
                    normalise("4", xnew, z["4"], t - 3, (zT_done["4"], pass_ready))
                if live(t - 2):
                    post_moments("C", POST, t - 2)
                soften(t, 4)
                if isinstance(t, int) and t == -1:
                    late_setup()
                if live(t - 2):
                    normalise("C", y["C"], z["C"], t - 2, (zT_done["C"], res_ready["3"]))
                if live(t - 4):
                    finish(t - 4, FFB)
                soften(t, 5)
                if live(t - 3):
                    gates(t - 3, (FFB, PROJ))
                if live(t):
                    heads_out("S", t)
                soften(t, 6)
                if live(t + 1):
                    spread_keys("S", t + 1)
                soften(t, 7)
                if live(t):
                    post_moments("S", POST, t)
                if live(t - 3):
                    route_best(t - 3)
                if live(t):
                    normalise("S", y["S"], z["S"], t, (zT_done["S"], res_ready["C"]))

            def drain(t):
                if live(t - 4):
                    route_weights(t - 4)
                if live(t - 3):
                    post_moments("3", FFB, t - 3)
                if live(t - 2):
                    heads_out("C", t - 2)
                if live(t - 3):
                    normalise("3", y["3"], z["3"], t - 3, (xnew_ready,))
                if live(t - 2):
                    post_moments("C", POST, t - 2)
                if live(t - 3):
                    dve.wait_ge(xnew_ready, t - 2)
                    moments("4", xnew, t - 3)
                if live(t - 2):
                    normalise("C", y["C"], z["C"], t - 2, (zT_done["C"], res_ready["3"]))
                if live(t - 3):
                    normalise("4", xnew, z["4"], t - 3, (zT_done["4"], pass_ready))
                if live(t - 4):
                    finish(t - 4, O_BANK)
                if live(t - 3):
                    route_best(t - 3)
                    gates(t - 3, S_BANK)

            run(dve, iteration, drain)

        @block.scalar
        def _(act):
            def load_weights():
                act.dma_start(const[:], const_d).then_inc(first_loaded, 16)
                act.dma_start(w["S"]["q"][:], wq_s).then_inc(proj_loaded["S"], 16)
                act.dma_start(w["S"]["v"][:], wv_s).then_inc(proj_loaded["S"], 16)
                act.dma_start(msk_s[:], mask_self).then_inc(mask_loaded, 16)
                nc.scalar.preload_act_table_set("exp_and_others")

            load_weights()

            def exponentials(t, c):
                ph, g, r = slot(t, c)
                if not live(g):
                    return
                b, back = parity(c), two_back(ph, g, r)
                act.wait_ge(shift_done[ph], ROWS * g + r + 1)
                nc.scalar.activation(prob[:, b, :], prob[:, b, :], ACT.Exp).then_inc(exp_done[ph], 1)

            def copy_probT(t, c):
                ph, g, r = slot(t, c)
                if not live(g):
                    return
                b, back = parity(c), two_back(ph, g, r)
                act.wait_ge(probT_done[ph], ROWS * g + r + 1)
                if back:
                    act.wait_ge(pv_done[back[0]], back[1])
                nc.scalar.activation(probT[:, b, :], PT_BANK[b][:], ACT.Copy).then_inc(probT_copied[ph], 1)

            def keys_queries(ph, g):
                bias = bqs[:, 0:1] if ph == "S" else bqs[:, 1:2]
                if isinstance(g, int) and g == 0:
                    act.wait_ge(dve_setup, 1)
                    act.wait_ge(pool_setup, 1 if ph == "S" else 2)
                act.wait_ge(qk_done[ph], g + 1)
                if follows(g):
                    act.wait_ge(kbd_ready[ph], g)
                nc.scalar.activation(kT[ph][:], PROJ[:, TOK:2 * TOK], ACT.Identity,
                                     bias=col("sa_bk" if ph == "S" else "ca_bk")).then_inc(kT_ready[ph], 1)
                if follows(g):
                    act.wait_ge(scores_done[ph], ROWS * g)
                for r in range(ROWS):
                    rg = slice(32 * r, 32 * r + 32)
                    last = nc.scalar.activation(qz[ph][rg, r, :], PROJ[rg, 0:TOK], ACT.Identity, bias=bias[rg],
                                                scale=SCALE)
                last.then_inc(q_ready[ph], 1)

            def values(ph, g):
                act.wait_ge(v_done[ph], g + 1)
                if follows(g):
                    act.wait_ge(pv_done[ph], ROWS * g)
                for h in range(2):
                    rng = slice(h * SEQ, (h + 1) * SEQ)
                    last = nc.scalar.activation(
                        vbd[ph][rng, :, :, h, 0:DK].rearrange("p b j d -> p (b j) d"),
                        POST2[rng, :].rearrange("p (b d) -> p b d", d=DK), ACT.Copy)
                last.then_inc(vbd_ready[ph], 1)

            def heads_fm(ph, g):
                act.wait_ge(oT_done[ph], g + 1)
                if follows(g):
                    act.wait_ge(y_done[ph], g)
                nc.scalar.activation(oT[ph][:], POST[:, 0:TOK], ACT.Identity,
                                     bias=col("sa_bv" if ph == "S" else "ca_bv")).then_inc(oT_ready[ph], 1)

            def to_fm(n, dst, g, used, gain=None, bias=None):
                act.wait_ge(zT_done[n], g + 1)
                for s in used:
                    if follows(g):
                        act.wait_ge(s, g)
                if gain is None:
                    nc.scalar.activation(dst[:], POST[:, 0:TOK], ACT.Copy).then_inc(zT_ready[n], 1)
                else:
                    nc.scalar.activation(dst[:], POST[:, 0:TOK], ACT.Identity, bias=col(bias),
                                         scale=col(gain)).then_inc(zT_ready[n], 1)

            def context_fm(g):
                act.wait_ge(encT_done, g + 1)
                if follows(g):
                    act.wait_ge(v_done["C"], g)
                nc.scalar.activation(encT[:], POST2, ACT.Copy).then_inc(encT_ready, 1)

            def hidden(half, g, psum):
                act.wait_ge(h_done[half], g + 1)
                if follows(g):
                    act.wait_ge(y_done["3"], g)
                for c in range(2):
                    last = nc.scalar.activation(hT[:, 2 * half + c, :], psum[:, c * TOK:(c + 1) * TOK], ACT.Relu,
                                                bias=col(f"ff{2 * half + c}"))
                last.then_inc(h_ready[half], 1)

            def mixture_fm(g, psum):
                act.wait_ge(zT_done["4"], g + 1)
                for s in (logits_done, gu_done[0], gu_done[1]):
                    if follows(g):
                        act.wait_ge(s, g)
                nc.scalar.activation(z4T[:, :, TAPS - 1:], psum.rearrange("p (b s) -> p b s", b=BATCH),
                                     ACT.Copy).then_inc(zT_ready["4"], 1)

            def scale_taps(g):
                act.wait_ge(zT_ready["4"], g + 1)
                if follows(g):
                    act.wait_ge(conv_step, g)
                for k in range(TAPS):
                    last = nc.scalar.activation(tapped[:, k, :].rearrange("p (b s) -> p b s", b=BATCH),
                                                z4T[:, :, k:k + SEQ], ACT.Identity, scale=col(f"tap{k}"))
                last.then_inc(tapped_ready, 1)

            def router_exp(g, psum):
                act.wait_ge(logits_done, g + 1)
                if follows(g):
                    act.wait_ge(cw_ready, g)
                nc.scalar.activation(e_r[:].rearrange("p a m -> p (a m)"), psum[:, 0:PAIRS * NE], ACT.Exp,
                                     scale=-1.0).then_inc(er_ready, 1)

            def gate_tanh(g, p, psum):
                act.wait_ge(gu_done[p], g + 1)
                if follows(g):
                    act.wait_ge(hid_ready[p], g)
                nc.scalar.activation(th[:, p], psum[:, 0:TOK], ACT.Tanh, scale=0.5).then_inc(th_ready[p], 1)

            def passes(g):
                act.wait_ge(cw_ready, g + 1)
                if follows(g):
                    act.wait_ge(rest_step, g)
                for p in range(PAIRS):
                    nc.scalar.activation(pass_x[:, p], z["4"][:, p], ACT.Copy, scale=c46[:, p:p + 1])
                    last = nc.scalar.activation(pass_r[:, p], z["4"][:, p], ACT.Relu, scale=cw[:, p, EXP + 3:EXP + 4])
                last.then_inc(pass_ready, 1)

            def hidden_fm(g):
                act.wait_ge(hidT_done, g + 1)
                if follows(g):
                    act.wait_ge(acc_done, g)
                nc.scalar.activation(hidT[:].rearrange("p a c t -> p (a c t)"), PROJ[:], ACT.Copy).then_inc(hidT_ready, 1)

            def iteration(t):
                copy_probT(t, -1)
                exponentials(t, 0)
                if live(t - 1):
                    to_fm("S", src_fm["C"], t - 1, (qk_done["C"],), "g1", "b1")
                    context_fm(t - 1)
                copy_probT(t, 0)
                exponentials(t, 1)
                if live(t - 1):
                    keys_queries("C", t - 1)
                copy_probT(t, 1)
                if live(t - 2):
                    heads_fm("C", t - 2)
                exponentials(t, 2)
                if live(t - 1):
                    values("C", t - 1)
                if live(t - 4):
                    hidden_fm(t - 4)
                copy_probT(t, 2)
                if live(t - 4):
                    passes(t - 4)
                exponentials(t, 3)
                copy_probT(t, 3)
                if live(t + 1):
                    to_fm("pre", src_fm["S"], t + 1, (v_done["S"],))
                if live(t - 3):
                    mixture_fm(t - 3, POST2)
                exponentials(t, 4)
                if live(t - 3):
                    gate_tanh(t - 3, 1, PROJ)
                copy_probT(t, 4)
                if live(t - 3):
                    gate_tanh(t - 3, 0, FFB)
                exponentials(t, 5)
                if live(t - 2):
                    to_fm("C", x2T, t - 2, (h_done[1],), "g2", "b2")
                if live(t - 3):
                    router_exp(t - 3, POST2)
                copy_probT(t, 5)
                if live(t - 2):
                    hidden(0, t - 2, FFB)
                if live(t + 1):
                    keys_queries("S", t + 1)
                if live(t):
                    heads_fm("S", t)
                if live(t + 1):
                    values("S", t + 1)
                exponentials(t, 6)
                if live(t - 3):
                    scale_taps(t - 3)
                copy_probT(t, 6)
                exponentials(t, 7)
                if live(t - 2):
                    hidden(1, t - 2, FFB)

            def drain(t):
                copy_probT(t, -1)
                if live(t - 4):
                    passes(t - 4)
                if live(t - 2):
                    heads_fm("C", t - 2)
                if live(t - 4):
                    hidden_fm(t - 4)
                if live(t - 2):
                    to_fm("C", x2T, t - 2, (h_done[1],), "g2", "b2")
                if live(t - 3):
                    mixture_fm(t - 3, PT_BANK[1][:, 0:TOK])
                    scale_taps(t - 3)
                if live(t - 2):
                    hidden(0, t - 2, FFB)
                if live(t - 3):
                    router_exp(t - 3, PT_BANK[0])
                if live(t - 2):
                    hidden(1, t - 2, PROJ)
                if live(t - 3):
                    gate_tanh(t - 3, 1, S_BANK[1])
                    gate_tanh(t - 3, 0, S_BANK[0])

            run(act, iteration, drain)

        @block.tensor
        def _(pe):
            mm = nc.tensor.matmul
            pe.wait_ge(first_loaded, 32)

            def scores(t, c):
                ph, g, r = slot(t, c)
                if not live(g):
                    return
                s, back = S_BANK[parity(c)], two_back(ph, g, r)
                if isinstance(g, int) and g == 0:
                    pe.wait_ge(dve_setup, 2)
                if ph == "C":
                    settle(pe)
                if back:
                    pe.wait_ge(shift_done[back[0]], back[1])
                if ph == "S":
                    mm(s[:].rearrange("p (h k) -> p h k", k=SEQ), pick_s[:],
                       neg_s[:].rearrange("p (h k) -> p h k", h=1).broadcast_to([SEQ, 8, SEQ]),
                       start=True, stop=False, skip_group_check=True)
                else:
                    for p in range(PAIRS):
                        mm(s[:, p * TOK:(p + 1) * TOK].rearrange("p (h k) -> p h k", k=SEQ), pick_c[:],
                           neg_c[:, g * PAIRS + p, :].rearrange("p (h k) -> p h k", h=1).broadcast_to([2, HR, SEQ])
                           if isinstance(g, int) else
                           neg_c[:, bass.ds(g * PAIRS + p, 1), :].broadcast_to([2, HR, SEQ]),
                           start=p == 0, stop=False, skip_group_check=True)
                if r == 0:
                    pe.wait_ge(q_ready[ph], g + 1)
                    pe.wait_ge(kbd_ready[ph], g + 1)
                for p in range(PAIRS):
                    for b in range(2):
                        tok = slice(p * P + b * SEQ, p * P + (b + 1) * SEQ)
                        last = mm(s[b * SEQ:(b + 1) * SEQ, p * TOK:(p + 1) * TOK].rearrange("p (h k) -> p h k", k=SEQ),
                                  qz[ph][:, r, tok], kbd[ph][:, :, tok], start=False, stop=True, skip_group_check=True)
                last.then_inc(scores_done[ph], 1)

            def turn_probs(t, c):
                ph, g, r = slot(t, c)
                if not live(g):
                    return
                b, back = parity(c), two_back(ph, g, r)
                pe.wait_ge(exp_done[ph], ROWS * g + r + 1)
                if back:
                    pe.wait_ge(probT_copied[back[0]], back[1])
                for j in range(4):
                    last = nc.tensor.transpose(PT_BANK[b][:, j * P:(j + 1) * P], prob[:, b, j * P:(j + 1) * P], ident)
                last.then_inc(probT_done[ph], 1)

            def heads(t, c):
                ph, g, r = slot(t, c)
                if not live(g):
                    return
                b, back = parity(c), two_back(ph, g, r)
                if r == 0:
                    pe.wait_ge(vbd_ready[ph], g + 1)
                    other = ("C", g - 2) if ph == "S" else ("S", g + 1)
                    if live(other[1]):
                        pe.wait_ge(o_ready[other[0]], other[1] + 1)
                    else:
                        if follows(g):
                            pe.wait_ge(o_ready[ph], g)
                pe.wait_ge(probT_copied[ph], ROWS * g + r + 1)
                for p in range(PAIRS):
                    for jj in range(2):
                        for sq in range(2):
                            j = 2 * r + jj
                            o = (p * HEADS + 2 * j) * VW
                            last = mm(O_BANK[sq * SEQ:(sq + 1) * SEQ, o:o + 2 * VW],
                                      probT[:, b, (2 * p + jj) * P + sq * SEQ:(2 * p + jj) * P + (sq + 1) * SEQ],
                                      vbd[ph][:, 2 * p + sq, j].rearrange("p h c -> p (h c)"),
                                      start=True, stop=True)
                last.then_inc(pv_done[ph], 1)

            def transpose_pairs(dst, src, s):
                for p in range(PAIRS):
                    last = nc.tensor.transpose(dst[:, p * P:(p + 1) * P], src[:, p], ident)
                last.then_inc(s, 1)

            def project_qk(ph, g, t, use):
                if isinstance(t, int):
                    pe.wait_ge(proj_loaded[ph], 48 if ph == "S" else 80)
                read = last_read(PROJ_USES, use, t)
                if read:
                    pe.wait_ge(*read)
                pe.wait_ge(zT_ready["pre" if ph == "S" else "S"], g + 1)
                if ph == "C":
                    pe.wait_ge(encT_ready, g + 1)
                mm(PROJ[:, 0:TOK], w[ph]["q"][:], src_fm[ph][:], start=True, stop=True)
                mm(PROJ[:, TOK:2 * TOK], w[ph]["k"][:], kv_fm[ph][:], start=True, stop=True).then_inc(qk_done[ph], 1)

            def project_v(ph, g, t, use):
                if isinstance(t, int):
                    pe.wait_ge(proj_loaded[ph], 48 if ph == "S" else 80)
                read = last_read(POST_USES, use, t)
                if read:
                    pe.wait_ge(*read)
                pe.wait_ge(zT_ready["pre"] if ph == "S" else encT_ready, g + 1)
                wv = w[ph]["v"][:].rearrange("p (j h d) -> p h j d", h=2, d=DK)
                for b in range(BATCH):
                    for h in range(2):
                        last = mm(POST2[h * SEQ:(h + 1) * SEQ, b * SEQ:(b + 1) * SEQ].rearrange("p (j d) -> p j d", d=DK),
                                  kv_fm[ph][:, b * SEQ:(b + 1) * SEQ], wv[:, h], start=True, stop=True)
                last.then_inc(v_done[ph], 1)

            def heads_to_fm(ph, g, t, use):
                read = last_read(POST_USES, use, t)
                if read:
                    pe.wait_ge(*read)
                pe.wait_ge(o_ready[ph], g + 1)
                transpose_pairs(POST, o_tm[ph], oT_done[ph])

            def output_product(ph, g, t, use):
                if isinstance(t, int):
                    pe.wait_ge(proj_loaded["C"], 80)
                read = last_read(POST_USES, use, t)
                if read:
                    pe.wait_ge(*read)
                pe.wait_ge(oT_ready[ph], g + 1)
                for p in range(PAIRS):
                    last = mm(POST[:, p * P:(p + 1) * P], oT[ph][:, p * P:(p + 1) * P], w[ph]["o"][:],
                              start=True, stop=True)
                last.then_inc(y_done[ph], 1)

            def z_to_fm(n, src, dst, uses, g, t, use):
                read = last_read(uses, use, t)
                if read:
                    pe.wait_ge(*read)
                pe.wait_ge(z_ready[n], g + 1)
                transpose_pairs(dst, src, zT_done[n])

            def context_to_fm(g, t, use):
                read = last_read(POST_USES, use, t)
                if read:
                    pe.wait_ge(*read)
                pe.wait_ge(ctx_loaded, 16 * (g + 1))
                transpose_pairs(POST2, ctx_tm, encT_done)

            def ffn_in(half, dst, uses, g, t, use):
                if isinstance(t, int):
                    pe.wait_ge(ffn_loaded, 32)
                read = last_read(uses, use, t)
                if read:
                    pe.wait_ge(*read)
                pe.wait_ge(zT_ready["C"], g + 1)
                for c in range(2):
                    k = 2 * half + c
                    last = mm(dst[:, c * TOK:(c + 1) * TOK], w1_sb[:, k * P:(k + 1) * P], x2T[:],
                              start=True, stop=True)
                last.then_inc(h_done[half], 1)

            def ffn_out(g, t, use):
                read = last_read(FFB_USES, use, t)
                if read:
                    pe.wait_ge(*read)
                pe.wait_ge(h_ready[1], g + 1)
                for p in range(PAIRS):
                    for k in range(FF):
                        last = mm(FFB[:, p * P:(p + 1) * P], hT[:, k, p * P:(p + 1) * P], w2_sb[:, k, :],
                                  start=k == 0, stop=k == FF - 1)
                last.then_inc(y_done["3"], 1)

            def tokens4(p, b):
                return z4T[:, 2 * p + b, TAPS - 1:TAPS - 1 + SEQ]

            def logits(dst, uses, g, t, use):
                if isinstance(t, int):
                    pe.wait_ge(mix_loaded, 64)
                read = last_read(uses, use, t)
                if read:
                    pe.wait_ge(*read)
                pe.wait_ge(zT_ready["4"], g + 1)
                for p in range(PAIRS):
                    for b in range(2):
                        last = mm(dst[b * SEQ:(b + 1) * SEQ, p * NE:(p + 1) * NE], tokens4(p, b), wr_sb[:],
                                  start=True, stop=True)
                last.then_inc(logits_done, 1)

            def gate_up(p, dst, uses, g, t, use):
                read = last_read(uses, use, t)
                if read:
                    pe.wait_ge(*read)
                pe.wait_ge(zT_ready["4"], g + 1)
                for b in range(2):
                    last = mm(dst[b * SEQ:(b + 1) * SEQ, :], tokens4(p, b),
                              wgu_sb[:].rearrange("p a e i -> p (a e i)"), start=True, stop=True)
                last.then_inc(gu_done[p], 1)

            def hidden_to_fm(g, t, use):
                read = last_read(PROJ_USES, use, t)
                if read:
                    pe.wait_ge(*read)
                for p in range(PAIRS):
                    pe.wait_ge(hidc_ready[p], g + 1)
                    for c in range(2):
                        last = nc.tensor.transpose(PROJ[:, (2 * p + c) * P:(2 * p + c + 1) * P],
                                                   hidc[:, p, c * P:(c + 1) * P], ident)
                last.then_inc(hidT_done, 1)

            def convolve(dst, uses, g, t, use):
                read = last_read(uses, use, t)
                if read:
                    pe.wait_ge(*read)
                pe.wait_ge(conv_ready, g + 1)
                for p in range(PAIRS):
                    mm(dst[:, p * P:(p + 1) * P], convT[:, p * P:(p + 1) * P], ident, start=p == 0, stop=False,
                       skip_group_check=True)

            def mix(dst, g):
                pe.wait_ge(hidT_ready, g + 1)
                for p in range(PAIRS):
                    for c in range(2):
                        last = mm(dst[:, p * P:(p + 1) * P], hidT[:, p, c, :], wd_sb[:, c, :], start=False,
                                  stop=c == 1, skip_group_check=True)
                last.then_inc(acc_done, 1)

            def iteration(t):
                scores(t, 0)
                turn_probs(t, -1)
                heads(t, -2)
                if live(t - 1):
                    context_to_fm(t - 1, t, 0)
                if live(t - 3):
                    ffn_out(t - 3, t, 0)
                if live(t - 1):
                    z_to_fm("S", z["S"], POST, POST_USES, t - 1, t, 0)
                scores(t, 1)
                turn_probs(t, 0)
                heads(t, -1)
                if live(t - 1):
                    project_qk("C", t - 1, t, 0)
                scores(t, 2)
                turn_probs(t, 1)
                heads(t, 0)
                if live(t - 1):
                    project_v("C", t - 1, t, 2)
                if live(t - 2):
                    heads_to_fm("C", t - 2, t, 2)
                scores(t, 3)
                if live(t - 4):
                    hidden_to_fm(t - 4, t, 1)
                    convolve(FFB, FFB_USES, t - 4, t, 1)
                turn_probs(t, 2)
                heads(t, 1)
                if live(t - 4):
                    mix(FFB, t - 4)
                if live(t - 2):
                    output_product("C", t - 2, t, 4)
                scores(t, 4)
                heads(t, 2)
                if live(t - 3):
                    z_to_fm("4", z["4"], POST2, POST_USES, t - 3, t, 5)
                turn_probs(t, 3)
                if live(t + 1):
                    z_to_fm("pre", xn, POST, POST_USES, t + 1, t, 5)
                scores(t, 5)
                heads(t, 3)
                turn_probs(t, 4)
                if live(t - 3):
                    gate_up(1, PROJ, PROJ_USES, t - 3, t, 2)
                    gate_up(0, FFB, FFB_USES, t - 3, t, 2)
                    logits(POST2, POST_USES, t - 3, t, 7)
                if live(t - 2):
                    z_to_fm("C", z["C"], POST, POST_USES, t - 2, t, 7)
                scores(t, 6)
                turn_probs(t, 5)
                if live(t - 2):
                    ffn_in(0, FFB, FFB_USES, t - 2, t, 3)
                if live(t + 1):
                    project_qk("S", t + 1, t, 3)
                heads(t, 4)
                if live(t + 1):
                    project_v("S", t + 1, t, 9)
                if live(t):
                    heads_to_fm("S", t, t, 9)
                scores(t, 7)
                if live(t):
                    output_product("S", t, t, 11)
                turn_probs(t, 6)
                if live(t - 2):
                    ffn_in(1, FFB, FFB_USES, t - 2, t, 4)
                heads(t, 5)

            def drain(t):
                scores(t, 0)
                heads(t, -2)
                scores(t, 1)
                turn_probs(t, -1)
                turn_probs(t, 0)
                if live(t - 3):
                    ffn_out(t - 3, t, 0)
                heads(t, -1)
                if live(t - 2):
                    heads_to_fm("C", t - 2, t, 0)
                    output_product("C", t - 2, t, 1)
                if live(t - 4):
                    pe.wait_ge(o_ready["C"], GROUPS)
                    convolve(O_BANK, SUM_USES, t - 4, t, 0)
                    hidden_to_fm(t - 4, t, 0)
                if live(t - 2):
                    z_to_fm("C", z["C"], POST, POST_USES, t - 2, t, 2)
                if live(t - 3):
                    z_to_fm("4", z["4"], PT_BANK[1], TOKEN_USES, t - 3, t, 0)
                if live(t - 4):
                    mix(O_BANK, t - 4)
                if live(t - 2):
                    ffn_in(0, FFB, FFB_USES, t - 2, t, 1)
                    ffn_in(1, PROJ, PROJ_USES, t - 2, t, 1)
                if live(t - 3):
                    logits(PT_BANK[0], LOGIT_USES, t - 3, t, 0)
                    gate_up(1, S_BANK[1], GATE_USES[1], t - 3, t, 0)
                    gate_up(0, S_BANK[0], GATE_USES[0], t - 3, t, 0)

            run(pe, iteration, drain)


def constants():
    import numpy as np

    c = np.zeros((P, C_END), np.float32)
    c[:, C_ID:C_ID + P] = np.eye(P)
    for p in range(P):
        c[p, C_HEAD + p % 32 // DK] = 1
    c[:, C_IOTA:C_IOTA + NE] = np.arange(NE)
    for b in range(2):
        c[b, C_PAIR + b * SEQ:C_PAIR + (b + 1) * SEQ] = 1
    c[:, C_POW:C_POW + PAIRS] = 0.5
    c[:, C_POW + PAIRS:C_END] = -0.5
    return c


def kernel(**inputs):
    import numpy as np
    import concourse.bacc as bacc
    from concourse.bass_utils import run_bass_kernel_spmd

    i = {k.replace("L0_xattn_", "").replace("L0_ffn_", ""): np.asarray(v) for k, v in inputs.items()}
    ff = i["ff_b1"].reshape(FF, P)
    taps = i["conv_w"].reshape(TAPS, P)
    per_partition = [i[n] for n in COLS[:10]] + [ff[k] for k in range(FF)] + [taps[k] for k in range(TAPS)]
    per_feature = [i[n] for n in ROWV]
    arrays = {
        "x": i["x"], "ctx": i["ctx_1024"], "mask_self": i["mask_SxS2_ik0"], "mask_cross": i["mask_Bx1x1xS2_if1"],
        "wq_s": i["sa_wq"], "wk_s": i["sa_wk"], "wv_s": i["sa_wv"], "wo_s": i["sa_wo"],
        "wq_c": i["ca_wq"], "wk_c": i["ca_wk"], "wv_c": i["ca_wv"], "wo_c": i["ca_wo"],
        "w1": i["ff_w1"], "w2": i["ff_w2"], "wr": i["Wr"], "wg": i["Wg"], "wu": i["Wu"], "wd": i["Wd"],
        "cols_d": np.stack(per_partition, axis=1), "rows_d": np.concatenate(per_feature)[None, :],
        "rb_d": i["router_bias"][None, :], "const_d": constants(),
    }
    nc = bacc.Bacc("TRN2", target_bir_lowering=False, num_devices=1)
    args = {}
    for name, a in arrays.items():
        arrays[name] = a = np.ascontiguousarray(a)
        args[name] = nc.dram_tensor(name, a.shape, mybir.dt.from_np(a.dtype), kind="ExternalInput").ap()
    args["out"] = nc.dram_tensor("out", i["x"].shape, F32, kind="ExternalOutput").ap()
    program(nc, **args)
    r = run_bass_kernel_spmd(nc, [arrays], core_ids=[0])
    return r.results[0]["out"]
```
